# Optimizing a Trainium2 kernel written in Bass

```python
import numpy as np
import jax
import jax.numpy as jnp

def _softmax(x, axis=-1):
    return jax.nn.softmax(x, axis=axis)

def _gelu(x):
    return jax.nn.gelu(x, approximate=True)

def _silu(x):
    return jax.nn.silu(x)

def _sigmoid(x):
    return jax.nn.sigmoid(x)

def _layernorm(x, axis=-1, eps=1e-05):
    m = jnp.mean(x, axis=axis, keepdims=True)
    v = jnp.var(x, axis=axis, keepdims=True)
    return (x - m) / jnp.sqrt(v + eps)

def _scatter_add(tgt, idx, src, axis=0):
    return tgt.at[idx].add(src)

def _segment_sum(src, seg, n):
    return jax.ops.segment_sum(src, seg, n)
kernel_name = 'mk_xattn_ffn_d1_seqx_r8_d6ad13'

def setup_inputs(seed: int=0):
    np.random.seed(seed)
    _w = jnp.asarray

    def _rec_inputs():
        import jax
        import jax.numpy as jnp
        _rk = jax.random.key(seed)
        x = -0.0002928 + 1 * jax.random.normal(jax.random.fold_in(_rk, 1), (2, 512, 128), jnp.float32)
        _lenS = 512 - jax.random.randint(jax.random.fold_in(_rk, 7), (2,), 0, max(1, 512 // 4) + 1, jnp.int32)
        _lenS2 = 77 - jax.random.randint(jax.random.fold_in(_rk, 8), (2,), 0, max(1, 77 // 4) + 1, jnp.int32)
        _ctx_1024P = jax.random.normal(jax.random.fold_in(_rk, 11), (2, 16, 128), jnp.float32)
        _ctx_1024c = jax.random.dirichlet(jax.random.fold_in(_rk, 511), 0.3 * jnp.ones((16,), jnp.float32), (2, 77))
        _ctx_1024t = jnp.einsum('bsk,bkd->bsd', _ctx_1024c, _ctx_1024P)
        _ctx_1024t = _ctx_1024t * jax.lax.rsqrt(jnp.mean(jnp.square(_ctx_1024t)) + 1e-12) * 0.953939
        ctx_1024 = -1.39393e-06 + 0.999914 * (_ctx_1024t + 0.3 * jax.random.normal(jax.random.fold_in(_rk, 611), (2, 77, 128), jnp.float32))
        _validS = jnp.arange(512)[None, :] < _lenS[:, None]
        _validS2 = jnp.arange(77)[None, :] < _lenS2[:, None]
        _causal = jnp.tril(jnp.ones((512, 512), dtype=bool))
        mask_BxSxS2_if1 = jnp.where(jnp.ones((2, 512, 77), dtype=bool), 1, 0).astype(jnp.int32)
        return (x, ctx_1024, mask_BxSxS2_if1)
    x, ctx_1024, mask_BxSxS2_if1 = _rec_inputs()

    def _L0_xattn_setup():
        import jax, jax.numpy as jnp
        import numpy as np
        EMB, HEADS = (128, 16)
        HEAD_DIM = EMB // HEADS

        def _linear(x, W, b):
            return jnp.einsum('bse,oe->bso', x, W) + b
        key = jax.random.key(seed)
        ks = jax.random.split(key, 11)
        B, S = (2, 256)
        sc = 1.0 / np.sqrt(EMB)
        inp = {'x': jax.random.normal(ks[0], (B, S, EMB), dtype=jnp.float32), 'y': jax.random.normal(ks[1], (B, S, EMB), dtype=jnp.float32), 'mask': jnp.ones((B, S, S), dtype=jnp.int32), 'Wq': jax.random.normal(ks[2], (EMB, EMB), dtype=jnp.float32) * sc, 'bq': jax.random.normal(ks[3], (EMB,), dtype=jnp.float32) * sc, 'Wk': jax.random.normal(ks[4], (EMB, EMB), dtype=jnp.float32) * sc, 'bk': jax.random.normal(ks[5], (EMB,), dtype=jnp.float32) * sc, 'Wv': jax.random.normal(ks[6], (EMB, EMB), dtype=jnp.float32) * sc, 'bv': jax.random.normal(ks[7], (EMB,), dtype=jnp.float32) * sc, 'Wo': jax.random.normal(ks[8], (EMB, EMB), dtype=jnp.float32) * sc, 'bo': jax.random.normal(ks[9], (EMB,), dtype=jnp.float32) * sc}
        return inp
    _L0_xattn_all = _L0_xattn_setup()
    _L0_xattn_in = {k: v for k, v in _L0_xattn_all.items() if k in ('Wq', 'bq', 'Wk', 'bk', 'Wv', 'bv', 'Wo', 'bo')}
    del _L0_xattn_all

    def _L0_ffn_setup():
        import jax, jax.numpy as jnp
        import numpy as np
        B, S, D, F, E, K = (2, 256, 128, 512, 8, 2)
        key = jax.random.key(seed)
        ks = jax.random.split(key, 5)
        x = jax.random.normal(ks[0], (B, S, D), dtype=jnp.float32)
        Wg = jax.random.normal(ks[1], (D, E), dtype=jnp.float32) * 0.02
        W1 = jax.random.normal(ks[2], (E, D, F), dtype=jnp.float32) * 0.02
        b1 = jnp.zeros((E, F), dtype=jnp.float32)
        W2 = jax.random.normal(ks[3], (E, F, D), dtype=jnp.float32) * 0.02
        b2 = jnp.zeros((E, D), dtype=jnp.float32)
        return {'x': x, 'Wg': Wg, 'W1': W1, 'b1': b1, 'W2': W2, 'b2': b2}
    _L0_ffn_all = _L0_ffn_setup()
    _L0_ffn_in = {k: v for k, v in _L0_ffn_all.items() if k in ('Wg', 'W1', 'b1', 'W2', 'b2')}
    del _L0_ffn_all
    return {'x': x, 'ctx_1024': ctx_1024, 'mask_BxSxS2_if1': mask_BxSxS2_if1, 'L0_xattn_Wq': _L0_xattn_in['Wq'], 'L0_xattn_bq': _L0_xattn_in['bq'], 'L0_xattn_Wk': _L0_xattn_in['Wk'], 'L0_xattn_bk': _L0_xattn_in['bk'], 'L0_xattn_Wv': _L0_xattn_in['Wv'], 'L0_xattn_bv': _L0_xattn_in['bv'], 'L0_xattn_Wo': _L0_xattn_in['Wo'], 'L0_xattn_bo': _L0_xattn_in['bo'], 'L0_ffn_Wg': _L0_ffn_in['Wg'], 'L0_ffn_W1': _L0_ffn_in['W1'], 'L0_ffn_b1': _L0_ffn_in['b1'], 'L0_ffn_W2': _L0_ffn_in['W2'], 'L0_ffn_b2': _L0_ffn_in['b2']}

def reference(x, ctx_1024, mask_BxSxS2_if1, L0_xattn_Wq, L0_xattn_bq, L0_xattn_Wk, L0_xattn_bk, L0_xattn_Wv, L0_xattn_bv, L0_xattn_Wo, L0_xattn_bo, L0_ffn_Wg, L0_ffn_W1, L0_ffn_b1, L0_ffn_W2, L0_ffn_b2):
    import jax
    import jax.numpy as jnp

    def _L0_xattn_ref(x, y, mask, Wq, bq, Wk, bk, Wv, bv, Wo, bo):
        import jax, jax.numpy as jnp
        import numpy as np
        EMB, HEADS = (128, 16)
        HEAD_DIM = EMB // HEADS

        def _linear(x, W, b):
            return jnp.einsum('bse,oe->bso', x, W) + b
        B, S, _ = x.shape
        q = _linear(x, Wq, bq).reshape(B, S, HEADS, HEAD_DIM).transpose(0, 2, 1, 3)
        k = _linear(y, Wk, bk).reshape(B, -1, HEADS, HEAD_DIM).transpose(0, 2, 1, 3)
        v = _linear(y, Wv, bv).reshape(B, -1, HEADS, HEAD_DIM).transpose(0, 2, 1, 3)
        score = jnp.einsum('bhqd,bhkd->bhqk', q, k) / jnp.sqrt(jnp.float32(HEAD_DIM))
        weights = jax.nn.softmax(score, axis=-1)
        attn = jnp.einsum('bhqk,bhkd->bhqd', weights, v)
        attn = attn.transpose(0, 2, 1, 3).reshape(B, S, EMB)
        return _linear(attn, Wo, bo)

    def _L0_ffn_ref(x, Wg, W1, b1, W2, b2):
        import jax, jax.numpy as jnp
        import numpy as np
        B, S, D, F, E, K = (2, 256, 128, 512, 8, 2)
        b, s, d = x.shape
        e = Wg.shape[1]
        T = b * s
        C = 2 * K * T // e
        xt = x.reshape(T, d)
        logits = xt.astype(jnp.float32) @ Wg.astype(jnp.float32)
        gates = jax.nn.softmax(logits, axis=-1)
        idx1 = jnp.argmax(gates, axis=-1)
        mask1 = jax.nn.one_hot(idx1, e, dtype=gates.dtype)
        gate1 = jnp.sum(gates * mask1, axis=-1)
        logits2 = jnp.where(mask1 > 0, -jnp.inf, logits)
        idx2 = jnp.argmax(logits2, axis=-1)
        mask2 = jax.nn.one_hot(idx2, e, dtype=gates.dtype)
        gate2 = jnp.sum(gates * mask2, axis=-1)
        denom = gate1 + gate2 + 1e-09
        w1 = gate1 / denom
        w2 = gate2 / denom
        p1 = jnp.cumsum(mask1, axis=0) - mask1
        pos1 = jnp.sum(p1 * mask1, axis=-1).astype(jnp.int32)
        off = jnp.sum(mask1, axis=0)
        p2 = jnp.cumsum(mask2, axis=0) - mask2 + off[None, :]
        pos2 = jnp.sum(p2 * mask2, axis=-1).astype(jnp.int32)
        keep1 = (pos1 < C).astype(xt.dtype)
        keep2 = (pos2 < C).astype(xt.dtype)
        pos1 = jnp.clip(pos1, 0, C - 1)
        pos2 = jnp.clip(pos2, 0, C - 1)
        xe = jnp.zeros((e, C, d), dtype=xt.dtype)
        xe = xe.at[idx1, pos1].add(xt * keep1[:, None])
        xe = xe.at[idx2, pos2].add(xt * keep2[:, None])
        h = jax.nn.gelu(jnp.einsum('ecd,edf->ecf', xe, W1) + b1[:, None, :], approximate=False)
        ye = jnp.einsum('ecf,efd->ecd', h, W2) + b2[:, None, :]
        out = ye[idx1, pos1] * (w1 * keep1)[:, None] + ye[idx2, pos2] * (w2 * keep2)[:, None]
        return out.reshape(b, s, d)
    x = x + _L0_xattn_ref(_layernorm(x, axis=-1), ctx_1024, mask_BxSxS2_if1, L0_xattn_Wq, L0_xattn_bq, L0_xattn_Wk, L0_xattn_bk, L0_xattn_Wv, L0_xattn_bv, L0_xattn_Wo, L0_xattn_bo)
    x = x + _L0_ffn_ref(_layernorm(x, axis=-1), L0_ffn_Wg, L0_ffn_W1, L0_ffn_b1, L0_ffn_W2, L0_ffn_b2)
    return x

_drawn_inputs = setup_inputs


def setup_inputs(seed=0):
    import zlib

    import numpy as np

    out = dict(_drawn_inputs(seed))
    spreads = {'L0_ffn_b1': (0.0, 0.558), 'L0_ffn_b2': (0.0, 0.1)}
    factors = {'L0_xattn_bk': 8.0}
    for name, (base, spread) in spreads.items():
        noise = np.random.default_rng([zlib.crc32(name.encode()), seed]).standard_normal(out[name].shape)
        drawn = base * np.exp(spread * noise) if base else spread * noise
        out[name] = jnp.asarray(drawn.astype(out[name].dtype))
    for name, factor in factors.items():
        out[name] = (out[name] * factor).astype(out[name].dtype)
    return out
```

```python
import concourse.bass as bass
from concourse import mybir
from contextlib import ExitStack


BATCH, SEQ, EMB = 2, 512, 128
KEYS = 77
HEADS = 16
HEAD_DIM = EMB // HEADS
EXPERTS = 8
HIDDEN = 512
TOP_K = 2
TOKENS = BATCH * SEQ
CAPACITY = 2 * TOP_K * TOKENS // EXPERTS
P = 128
TILES = TOKENS // P
TILES_PER_BATCH = SEQ // P
FLAT = HEADS * KEYS
CHUNKS = -(-FLAT // P)
LAST_ROWS = FLAT - (CHUNKS - 1) * P
SPAN = 3
FIRST_HEAD = [min(c * P // KEYS, HEADS - SPAN) for c in range(CHUNKS)]
VW = HEAD_DIM + 1
GROUPS = [(0, 6), (6, 12), (12, 16)]
QUADS = [(0, 4), (4, 8), (8, CHUNKS)]
HCH = HIDDEN // P
HALVES = TOKENS // 512
STEPS = HALVES * HCH
LN_EPS = 1e-5
BIG = 3.0e38

PAR_A = [("wk", EMB), ("ctx", BATCH * KEYS), ("wv", EMB), ("bk", 1), ("bq", 1)]
PAR_B = [("wq", EMB), ("wo", EMB), ("wg", EXPERTS), ("b1", EXPERTS * HCH)]
CONST = [("ident", P), ("head", HEADS), ("vmask", CHUNKS * SPAN), ("upper", P), ("rank", EXPERTS)]


def columns(parts):
    at, out = 0, {}
    for name, width in parts:
        out[name] = (at, at + width)
        at += width
    return out, at


def xattn_moe(nc, x, par_a, par_b, bias_v, bias_o, w1, w2, b2, const, out):
    f32, f32r, bf16 = mybir.dt.float32, mybir.dt.float32r, mybir.dt.bfloat16
    ALU, ACT, AX = mybir.AluOpType, mybir.ActivationFunctionType, mybir.AxisListType
    SCALE = float(HEAD_DIM) ** -0.5
    col_a, width_a = columns(PAR_A)
    col_b, width_b = columns(PAR_B)
    col_c, width_c = columns(CONST)

    ctx = ExitStack()
    with ctx:
        def sb(name, shape, dt=f32):
            return ctx.enter_context(nc.sbuf_tensor(name, shape, dt))

        def sem(name):
            return ctx.enter_context(nc.semaphore(name))

        pa = sb("pa", [P, width_a])
        pb = sb("pb", [P, width_b])
        cst = sb("cst", [P, width_c])

        def A(name):
            return pa[:, col_a[name][0]:col_a[name][1]]

        def B(name):
            return pb[:, col_b[name][0]:col_b[name][1]]

        def C(name):
            return cst[:, col_c[name][0]:col_c[name][1]]

        X = sb("X", [P, TILES, EMB])
        bv_all = sb("bv_all", [P, CHUNKS * SPAN * HEAD_DIM])
        bo_all = sb("bo_all", [P, EMB])
        b2_sb = sb("b2_sb", [EXPERTS, EMB])
        X1 = sb("X1", [P, TILES, EMB])
        eps = sb("eps", [P, 1])
        neg_half = sb("neg_half", [P, TILES])
        stats = sb("stats", [P, TILES, 6])
        mv = sb("mv", [P, TILES, 2])
        rstd = sb("rstd", [P, TILES])
        negm = sb("negm", [P, TILES])
        xn = sb("xn", [P, TILES, EMB])
        xnT = sb("xnT", [P, TOKENS])
        q_hi = sb("q_hi", [P, TOKENS], f32r)
        q_lo = sb("q_lo", [P, TOKENS], f32r)
        kt_hi = sb("kt_hi", [P, BATCH, KEYS], f32r)
        kt_lo = sb("kt_lo", [P, BATCH, KEYS], f32r)
        kb_hi = sb("kb_hi", [P, BATCH, FLAT], f32r)
        kb_lo = sb("kb_lo", [P, BATCH, FLAT], f32r)
        ctx_rep = sb("ctx_rep", [P, BATCH, FLAT])
        v_first = sb("v_first", [P, BATCH, HEADS * VW])
        v_rest = sb("v_rest", [P, BATCH, CHUNKS, SPAN * VW])
        v_sum = sb("v_sum", [P, BATCH, CHUNKS, SPAN * HEAD_DIM])
        mx = sb("mx", [P, 2, HEADS])
        shifted = sb("shifted", [P, 2, CHUNKS * P])
        probs = sb("probs", [P, 2, CHUNKS * P])
        rec = sb("rec", [P, 2, HEADS])
        attn = sb("attn", [P, 2, EMB])
        attnT = sb("attnT", [P, 2, EMB])
        stats2 = sb("stats2", [P, 2, 6])
        mv2 = sb("mv2", [P, 2, 2])
        ln2 = sb("ln2", [P, 2, 3])
        xn2 = sb("xn2", [P, 2, EMB])
        x2_hi = sb("x2_hi", [P, TOKENS], f32r)
        x2_lo = sb("x2_lo", [P, TOKENS], f32r)
        wg_hi = sb("wg_hi", [P, EXPERTS], f32r)
        wg_lo = sb("wg_lo", [P, EXPERTS], f32r)
        ones_bf = sb("ones_bf", [P, P], bf16)
        upper_bf = sb("upper_bf", [P, P], bf16)
        TE = TILES * EXPERTS
        r_l = sb("r_l", [P, TE])
        r_e = sb("r_e", [P, TE])
        r_g = sb("r_g", [P, TE])
        r_a = sb("r_a", [P, TE])
        r_b = sb("r_b", [P, TE])
        r_m = sb("r_m", [P, 2, TE])
        r_mb = sb("r_mb", [P, 2, TE], bf16)
        r_before = sb("r_before", [P, 2, TILES, EXPERTS], bf16)
        r_s = sb("r_s", [P, 8, TILES])
        r_pm = sb("r_pm", [P, 2, TE])
        r_pos = sb("r_pos", [P, 2, TILES])
        r_w = sb("r_w", [P, 2, TILES])
        r_wm = sb("r_wm", [P, 2, TE])
        gate = sb("gate", [P, TE])
        gateT = sb("gateT", [EXPERTS, TOKENS])
        gate_all = sb("gate_all", [P, EXPERTS, TOKENS])
        w1_raw = sb("w1_raw", [P, 2, HIDDEN])
        w2_raw = sb("w2_raw", [P, 2, HCH * EMB])
        w1_hi = sb("w1_hi", [P, 2, HIDDEN], f32r)
        w1_lo = sb("w1_lo", [P, 2, HIDDEN], f32r)
        w2_hi = sb("w2_hi", [P, 2, HCH * EMB], f32r)
        w2_lo = sb("w2_lo", [P, 2, HCH * EMB], f32r)
        RING = 4
        b1_pair = sb("b1_pair", [P, 2 * HCH])
        h_hi = sb("h_hi", [P, RING, 512], f32r)
        h_lo = sb("h_lo", [P, RING, 512], f32r)
        y_gated = sb("y_gated", [P, 2, 512])
        y_sum = sb("y_sum", [P, TOKENS])
        result = sb("result", [P, TILES, EMB])

        bank = [ctx.enter_context(nc.psum_tensor(f"bank{i}", [P, 512], f32)) for i in range(8)]
        score_bank = bank[0:3]
        turned_bank = bank[3:5]
        out_bank, proj_bank, xn2_bank = bank[5:8]
        hidden_bank = bank[0:4]
        y_bank = bank[4:6]
        final_bank = bank[6:8]

        ld_pa, ld_pb, ld_cst, ld_x, ld_bv, ld_bo, ld_b2 = (
            sem(n) for n in ("ld_pa", "ld_pb", "ld_cst", "ld_x", "ld_bv", "ld_bo", "ld_b2"))
        pool_chain, dve_chain = sem("pool_chain"), sem("dve_chain")
        consts_set, zeros_set = sem("consts_set"), sem("zeros_set")
        keys_projected, kt_hi_done, kt_done, kb_done = (
            sem(n) for n in ("keys_projected", "kt_hi_done", "kt_done", "kb_done"))
        ctx_copied, values_projected, values_set = (
            sem(n) for n in ("ctx_copied", "values_projected", "values_set"))
        moments_done, rstd_done, normed, norm_turned, norm_copied = (
            sem(n) for n in ("moments_done", "rstd_done", "normed", "norm_turned", "norm_copied"))
        q_projected, q_hi_done, q_done, bo_added = (
            sem(n) for n in ("q_projected", "q_hi_done", "q_done", "bo_added"))
        scored, max_done, shift_done, turned, exp_done = (
            sem(n) for n in ("scored", "max_done", "shift_done", "turned", "exp_done"))
        weighted, rec_done, attn_done, attn_turned, attn_copied = (
            sem(n) for n in ("weighted", "rec_done", "attn_done", "attn_turned", "attn_copied"))
        projected, x1_done, stats2_done, moments2_done, xn2_done = (
            sem(n) for n in ("projected", "x1_done", "stats2_done", "moments2_done", "xn2_done"))
        xn2_turned, x2_hi_done, x2_done, wg_done = (
            sem(n) for n in ("xn2_turned", "x2_hi_done", "x2_done", "wg_done"))
        logits_done, logits_shifted, gates_exp, masks_done, ranked, gate_done, gate_turned, gateT_done = (
            sem(n) for n in ("logits_done", "logits_shifted", "gates_exp", "masks_done", "ranked",
                             "gate_done", "gate_turned", "gateT_done"))
        gate_spread = sem("gate_spread")
        ld_x2, stats_done, upper_set, v_sum_done, w_hi_done, before_zero = (
            sem(n) for n in ("ld_x2", "stats_done", "upper_set", "v_sum_done", "w_hi_done", "before_zero"))
        w1_loaded = [sem("w1_loaded0"), sem("w1_loaded1")]
        w2_loaded = [sem("w2_loaded0"), sem("w2_loaded1")]
        w1_split, w2_split = sem("w1_split"), sem("w2_split")
        up_done, gelu_done, h_hi_done, h_done, down_done = (
            sem(n) for n in ("up_done", "gelu_done", "h_hi_done", "h_done", "down_done"))
        y_gated_done, y_added = (sem(n) for n in ("y_gated_done", "y_added"))
        final_done, result_done, stored = (sem(n) for n in ("final_done", "result_done", "stored"))

        gate_stored, b1_here, slot_ready = (sem(n) for n in ("gate_stored", "b1_here", "slot_ready"))
        gate_rows = nc.dram_tensor("gate_rows", (EXPERTS, TOKENS), f32, kind="Internal").ap()
        x_v = x.rearrange("(t p) e -> p t e", p=P)
        out_v = out.rearrange("(t p) e -> p t e", p=P)
        w1_v = w1.rearrange("e d f -> d e f")
        w2_v = w2.rearrange("e (c p) d -> p e c d", p=P)
        HT = TILES // 2

        block = ctx.enter_context(nc.Block())

        @block.sync
        def _(sp):
            sp.dma_start(pa[:], par_a).then_inc(ld_pa, 16)
            sp.dma_start(X[:, 0:HT, :], x_v[:, 0:HT, :]).then_inc(ld_x, 16)
            sp.dma_start(cst[:], const).then_inc(ld_cst, 16)
            sp.dma_start(pb[:], par_b).then_inc(ld_pb, 16)

            def load_expert(e, u):
                sp.dma_start(w1_raw[:, u, :], w1_v[:, e, :]).then_inc(w1_loaded[u], 16)
                sp.dma_start(w2_raw[:, u, :].rearrange("p (c d) -> p c d", c=HCH),
                             w2_v[:, e, :, :]).then_inc(w2_loaded[u], 16)

            for e in range(2):
                load_expert(e, e)
            with sp.Fori(1, EXPERTS // 2) as i:
                for u in range(2):
                    sp.wait_ge(w1_split, i * 2 + (u - 1))
                    sp.wait_ge(w2_split, i * 2 + (u - 1))
                    sp.dma_start(w1_raw[:, u, :], w1_v[:, bass.ds(i * 2 + u, 1), :]
                                 .rearrange("p a f -> p (a f)")).then_inc(w1_loaded[u], 16)
                    sp.dma_start(w2_raw[:, u, :].rearrange("p (c d) -> p c d", c=HCH),
                                 w2_v[:, bass.ds(i * 2 + u, 1), :, :]
                                 .rearrange("p a c d -> p (a c) d")).then_inc(w2_loaded[u], 16)
            for s in range(HALVES):
                sp.wait_ge(result_done, HT * (s + 1))
                sp.dma_start(out_v[:, s * HT:(s + 1) * HT, :],
                             result[:, s * HT:(s + 1) * HT, :]).then_inc(stored, 16)
            sp.wait_ge(stored, 16 * HALVES)

        @block.gpsimd
        def _(pool):
            chain = [0]

            def link(ins):
                chain[0] += 1
                ins.then_inc(pool_chain, 1)
                pool.wait_ge(pool_chain, chain[0])

            nc.gpsimd.memset(eps[:], LN_EPS).then_inc(consts_set, 1)
            nc.gpsimd.memset(neg_half[:], -0.5).then_inc(consts_set, 1)
            nc.gpsimd.memset(ones_bf[:], 1.0).then_inc(consts_set, 1)
            nc.gpsimd.memset(v_first[:], 0.0).then_inc(zeros_set, 1)
            nc.gpsimd.memset(shifted[:, :, FLAT:CHUNKS * P], 0.0).then_inc(zeros_set, 1)
            nc.gpsimd.memset(y_sum[:], 0.0).then_inc(zeros_set, 1)
            pool.wait_ge(ld_pa, 16)
            for b in range(BATCH):
                c = A("ctx")[:, b * KEYS:(b + 1) * KEYS]
                nc.gpsimd.tensor_copy(
                    ctx_rep[:, b, :].rearrange("p (h k) -> p h k", h=HEADS),
                    c.unsqueeze(1).broadcast_to([P, HEADS, KEYS])).then_inc(ctx_copied, 1)

            pool.wait_ge(consts_set, 3)
            for s in range(2):
                pool.wait_ge(moments_done, HT * (s + 1))
                sl = slice(s * HT, (s + 1) * HT)
                link(nc.gpsimd.tensor_scalar(rstd[:, sl], mv[:, sl, 1], LN_EPS, None, ALU.add))
                nc.gpsimd.tensor_tensor(rstd[:, sl], rstd[:, sl], neg_half[:, sl], ALU.pow)\
                    .then_inc(rstd_done, 1)

            pool.wait_ge(ld_cst, 16)
            pool.wait_ge(kt_done, 1)
            for h in range(HEADS):
                nc.gpsimd.tensor_scalar(kb_lo[:, :, h * KEYS:(h + 1) * KEYS], kt_lo[:].bitcast(f32),
                                        C("head")[:, h:h + 1], 1.0, ALU.mult, ALU.mult)\
                    .then_inc(kb_done, 1)

            pool.wait_ge(ld_pb, 16)
            link(nc.gpsimd.tensor_copy(wg_hi[:], B("wg")))
            nc.gpsimd.tensor_tensor(wg_lo[:], B("wg"), wg_hi[:].bitcast(f32), ALU.subtract)\
                .then_inc(wg_done, 1)

            def split(n, u, raw, hi, lo, loaded, level, signal):
                pool.wait_ge(loaded[u], level)
                pool.sem_inc(slot_ready, 1)
                link_hi = nc.gpsimd.tensor_copy(hi[:, u, :], raw[:, u, :])
                link_hi.then_inc(w_hi_done, 1)
                pool.wait_ge(w_hi_done, n)
                nc.gpsimd.tensor_tensor(lo[:, u, :], raw[:, u, :], hi[:, u, :].bitcast(f32),
                                        ALU.subtract).then_inc(signal, 1)

            for e in range(2):
                split(2 * e + 1, e, w1_raw, w1_hi, w1_lo, w1_loaded, 16, w1_split)
                split(2 * e + 2, e, w2_raw, w2_hi, w2_lo, w2_loaded, 16, w2_split)

            for t in range(TILES):
                p = t % 2
                pool.wait_ge(moments2_done, t + 1)
                link(nc.gpsimd.tensor_scalar(ln2[:, p, 0:1], mv2[:, p, 1:2], LN_EPS, None, ALU.add))
                link(nc.gpsimd.tensor_scalar(ln2[:, p, 1:2], mv2[:, p, 0:1], -1.0, None, ALU.mult))
                link(nc.gpsimd.tensor_tensor(ln2[:, p, 2:3], ln2[:, p, 0:1], neg_half[:, 0:1], ALU.pow))
                if t >= 2:
                    pool.wait_ge(xn2_turned, t - 1)
                nc.gpsimd.tensor_scalar(xn2[:, p, :], X1[:, t, :], ln2[:, p, 1:2], ln2[:, p, 2:3],
                                        ALU.add, ALU.mult).then_inc(xn2_done, 1)

            def add_up(m, s):
                pool.wait_ge(y_gated_done, m + 1)
                half = y_sum[:, s * 512:(s + 1) * 512]
                nc.gpsimd.tensor_tensor(half, half, y_gated[:, s, :], ALU.add).then_inc(y_added, 1)

            pool.wait_ge(zeros_set, 3)
            with pool.Fori(0, EXPERTS // 2 - 1) as i:
                for u in range(2):
                    for s in range(HALVES):
                        add_up(i * 4 + (2 * u + s), s)
                    pool.wait_ge(up_done, i * (2 * STEPS) + STEPS * (u + 1))
                    split(i * 4 + (5 + 2 * u), u, w1_raw, w1_hi, w1_lo, w1_loaded, i * 16 + 32, w1_split)
                    pool.wait_ge(down_done, i * (2 * STEPS) + STEPS * (u + 1))
                    split(i * 4 + (6 + 2 * u), u, w2_raw, w2_hi, w2_lo, w2_loaded, i * 16 + 32, w2_split)
            for m in range(2 * EXPERTS - 4, 2 * EXPERTS):
                add_up(m, m % 2)

        @block.scalar
        def _(act):
            act.dma_start(X[:, HT:TILES, :], x_v[:, HT:TILES, :]).then_inc(ld_x2, 16)
            act.dma_start(bv_all[:], bias_v.partition_broadcast(P)).then_inc(ld_bv, 16)
            act.dma_start(bo_all[:], bias_o.partition_broadcast(P)).then_inc(ld_bo, 16)
            act.dma_start(b2_sb[:], b2).then_inc(ld_b2, 16)
            for s in range(2):
                act.wait_ge(norm_turned, s + 1)
                nc.scalar.activation(xnT[:, s * 512:(s + 1) * 512], bank[3 + s][:], ACT.Copy)\
                    .then_inc(norm_copied, 1)
            for s in range(2):
                act.wait_ge(q_projected, s + 1)
                nc.scalar.activation(q_hi[:, s * 512:(s + 1) * 512], bank[s][:], ACT.Identity,
                                     bias=A("bq")).then_inc(q_hi_done, 1)

            def exps(t):
                for j, (c0, c1) in enumerate(QUADS):
                    u = 3 * t + j
                    act.wait_ge(turned, u + 1)
                    if t >= 2 and j == 0:
                        act.wait_ge(weighted, t - 1)
                    nc.scalar.activation(probs[:, t % 2, c0 * P:c1 * P],
                                         turned_bank[u % 2][:, 0:(c1 - c0) * P], ACT.Exp,
                                         scale=SCALE).then_inc(exp_done, 1)

            def copy_attn(t):
                act.wait_ge(attn_turned, t + 1)
                nc.scalar.activation(attnT[:, t % 2, :], proj_bank[:, 0:P], ACT.Copy)\
                    .then_inc(attn_copied, 1)

            def copy_xn2(t):
                act.wait_ge(xn2_turned, t + 1)
                nc.scalar.activation(x2_hi[:, t * P:(t + 1) * P], xn2_bank[:, 0:P], ACT.Copy)\
                    .then_inc(x2_hi_done, 1)

            for k in range(TILES + 4):
                if 0 <= k - 3 < TILES:
                    copy_attn(k - 3)
                if 0 <= k - 1 < TILES:
                    exps(k - 1)
                if 0 <= k - 4 < TILES:
                    copy_xn2(k - 4)

            act.wait_ge(logits_shifted, 1)
            nc.scalar.activation(r_e[:], r_l[:], ACT.Exp).then_inc(gates_exp, 1)
            for s in range(2):
                act.wait_ge(gate_turned, s + 1)
                nc.scalar.activation(gateT[:, s * 512:(s + 1) * 512], final_bank[s][0:EXPERTS, :],
                                     ACT.Copy).then_inc(gateT_done, 1)
            act.wait_ge(gateT_done, 2)
            act.dma_start(gate_rows, gateT[:]).then_inc(gate_stored, 16)
            act.wait_ge(gate_stored, 16)
            for e in range(EXPERTS):
                act.dma_start(gate_all[:, e, :], gate_rows[e, :].partition_broadcast(P))\
                    .then_inc(gate_spread, 16)

            def hidden(n, j, c, r, first):
                act.wait_ge(up_done, n + 1)
                nc.scalar.activation(hidden_bank[r][:], hidden_bank[r][:], ACT.Gelu,
                                     bias=b1_pair[:, j // STEPS * HCH + c:j // STEPS * HCH + c + 1]).then_inc(gelu_done, 1)
                act.wait_ge(gelu_done, n + 1)
                if not first:
                    act.wait_ge(down_done, n - (RING - 1))
                nc.scalar.activation(h_hi[:, r, :], hidden_bank[r][:], ACT.Copy).then_inc(h_hi_done, 1)

            def pair(i, first):
                nc.scalar.activation(b1_pair[:], pb[:, bass.ds(i * (2 * HCH) + col_b["b1"][0], 2 * HCH)],
                                     ACT.Copy).then_inc(b1_here, 1)
                act.wait_ge(b1_here, i + 1)
                for j in range(2 * STEPS):
                    hidden(i * (2 * STEPS) + j, j, j % HCH, j % RING, first and j < RING)

            act.wait_ge(ld_pb, 16)
            pair(0, True)
            with act.Fori(1, EXPERTS // 2) as i:
                pair(i, False)

        @block.vector
        def _(dve):
            chain = [0]

            def link(ins):
                chain[0] += 1
                ins.then_inc(dve_chain, 1)
                dve.wait_ge(dve_chain, chain[0])

            def bc(ap, shape):
                return ap.broadcast_to(shape)

            for t in range(TILES):
                dve.wait_ge(ld_x if t < HT else ld_x2, 16)
                nc.vector.bn_stats(stats[:, t, :], X[:, t, :]).then_inc(stats_done, 1)
            for t in range(TILES):
                dve.wait_ge(stats_done, t + 1)
                nc.vector.bn_aggr(mv[:, t, :], stats[:, t, :]).then_inc(moments_done, 1)

            dve.wait_ge(keys_projected, 1)
            kt = bank[6][:, 0:BATCH * KEYS].rearrange("p (b k) -> p b k", b=BATCH)
            nc.vector.tensor_scalar(kt_hi[:], kt, A("bk"), None, ALU.add).then_inc(kt_hi_done, 1)
            dve.wait_ge(kt_hi_done, 1)
            nc.vector.scalar_tensor_tensor(out=kt_lo[:], in0=kt, scalar=A("bk"), in1=kt_hi[:].bitcast(f32),
                                           op0=ALU.add, op1=ALU.subtract).then_inc(kt_done, 1)

            for s in range(2):
                dve.wait_ge(rstd_done, s + 1)
                for t in range(s * HT, (s + 1) * HT):
                    nc.vector.tensor_scalar(xn[:, t, :], X[:, t, :], mv[:, t, 0:1], rstd[:, t:t + 1],
                                            ALU.subtract, ALU.mult).then_inc(normed, 1)

            dve.wait_ge(ld_cst, 16)
            for h in range(HEADS):
                nc.vector.tensor_scalar(kb_hi[:, :, h * KEYS:(h + 1) * KEYS], kt_hi[:].bitcast(f32),
                                        C("head")[:, h:h + 1], None, ALU.mult).then_inc(kb_done, 1)
            nc.vector.tensor_copy(upper_bf[:], C("upper")).then_inc(upper_set, 1)

            dve.wait_ge(values_projected, 1)
            dve.wait_ge(ld_bv, 16)
            for b in range(BATCH):
                n = CHUNKS * SPAN * HEAD_DIM
                for lo_, hi_, rows in ((0, n - SPAN * HEAD_DIM, P), (n - SPAN * HEAD_DIM, n, LAST_ROWS)):
                    last = nc.vector.tensor_tensor(
                        v_sum[0:rows, b].rearrange("p c w -> p (c w)")[:, lo_:hi_],
                        bank[7][0:rows, b * n + lo_:b * n + hi_], bv_all[0:rows, lo_:hi_], ALU.add)
                    last.then_inc(v_sum_done, 1)
            dve.wait_ge(v_sum_done, 2 * BATCH)
            dve.wait_ge(zeros_set, 1)
            vmask = C("vmask").rearrange("p (c j) -> p c j", c=CHUNKS)
            for b in range(BATCH):
                v4 = v_rest[:, b].rearrange("p c (j w) -> p c j w", j=SPAN)
                s4 = v_sum[:, b].rearrange("p c (j w) -> p c j w", j=SPAN)
                m4 = vmask.unsqueeze(3)
                for c0, c1, rows in ((0, CHUNKS - 1, P), (CHUNKS - 1, CHUNKS, LAST_ROWS)):
                    nc.vector.tensor_tensor(v4[0:rows, c0:c1, :, 0:HEAD_DIM], s4[0:rows, c0:c1],
                                            bc(m4[0:rows, c0:c1], [rows, c1 - c0, SPAN, HEAD_DIM]),
                                            ALU.mult).then_inc(values_set, 1)
                nc.vector.tensor_copy(v4[:, :, :, HEAD_DIM], vmask).then_inc(values_set, 1)
            dve.wait_ge(values_set, 3 * BATCH)
            nc.vector.tensor_copy(v_first[:, :, 0:SPAN * VW], v_rest[:, :, 0, :]).then_inc(values_set, 1)

            for s in range(2):
                dve.wait_ge(q_hi_done, s + 1)
                nc.vector.scalar_tensor_tensor(
                    out=q_lo[:, s * 512:(s + 1) * 512], in0=bank[s][:], scalar=A("bq"),
                    in1=q_hi[:, s * 512:(s + 1) * 512].bitcast(f32),
                    op0=ALU.add, op1=ALU.subtract).then_inc(q_done, 1)
            dve.wait_ge(ld_bo, 16)
            nc.vector.tensor_tensor(X[:], X[:], bc(bo_all[:].unsqueeze(1), [P, TILES, EMB]), ALU.add)\
                .then_inc(bo_added, 1)
            dve.wait_ge(bo_added, 1)
            dve.wait_ge(zeros_set, 2)

            def maximum(t, g):
                h0, h1 = GROUPS[g]
                dve.wait_ge(scored, 3 * t + g + 1)
                s = score_bank[g][:, 0:(h1 - h0) * KEYS].rearrange("p (h k) -> p h k", k=KEYS)
                nc.vector.tensor_reduce(mx[:, t % 2, h0:h1], s, AX.X, ALU.max).then_inc(max_done, 1)

            def shift(t, g):
                h0, h1 = GROUPS[g]
                dve.wait_ge(max_done, 3 * t + g + 1)
                if t >= 2 and g == 0:
                    dve.wait_ge(turned, 3 * (t - 1))
                s = score_bank[g][:, 0:(h1 - h0) * KEYS].rearrange("p (h k) -> p h k", k=KEYS)
                o = shifted[:, t % 2, h0 * KEYS:h1 * KEYS].rearrange("p (h k) -> p h k", k=KEYS)
                m = mx[:, t % 2, h0:h1].unsqueeze(2)
                nc.vector.tensor_tensor(o, s, bc(m, [P, h1 - h0, KEYS]), ALU.subtract)\
                    .then_inc(shift_done, 1)

            def divide(t):
                dve.wait_ge(weighted, t + 1)
                o = out_bank[:, 0:HEADS * VW].rearrange("p (h w) -> p h w", w=VW)
                nc.vector.reciprocal(rec[:, t % 2, :], o[:, :, HEAD_DIM]).then_inc(rec_done, 1)
                dve.wait_ge(rec_done, t + 1)
                if t >= 2:
                    dve.wait_ge(attn_turned, t - 1)
                nc.vector.tensor_tensor(
                    attn[:, t % 2, :].rearrange("p (h d) -> p h d", h=HEADS), o[:, :, 0:HEAD_DIM],
                    bc(rec[:, t % 2, :].unsqueeze(2), [P, HEADS, HEAD_DIM]), ALU.mult)\
                    .then_inc(attn_done, 1)

            def residual(t):
                dve.wait_ge(projected, t + 1)
                nc.vector.tensor_tensor(X1[:, t, :], proj_bank[:, 0:P], X[:, t, :], ALU.add)\
                    .then_inc(x1_done, 1)
                dve.wait_ge(x1_done, t + 1)
                nc.vector.bn_stats(stats2[:, t % 2, :], X1[:, t, :]).then_inc(stats2_done, 1)
                dve.wait_ge(stats2_done, t + 1)
                if t >= 2:
                    dve.wait_ge(xn2_done, t - 1)
                nc.vector.bn_aggr(mv2[:, t % 2, :], stats2[:, t % 2, :]).then_inc(moments2_done, 1)

            def low_xn2(t):
                dve.wait_ge(x2_hi_done, t + 1)
                nc.vector.tensor_tensor(x2_lo[:, t * P:(t + 1) * P], xn2_bank[:, 0:P],
                                        x2_hi[:, t * P:(t + 1) * P].bitcast(f32), ALU.subtract)\
                    .then_inc(x2_done, 1)

            for k in range(TILES + 4):
                if k < TILES:
                    maximum(k, 0)
                    maximum(k, 1)
                    shift(k, 0)
                if 0 <= k - 3 < TILES:
                    residual(k - 3)
                if k < TILES:
                    maximum(k, 2)
                    shift(k, 1)
                    shift(k, 2)
                if 0 <= k - 2 < TILES:
                    divide(k - 2)
                if 0 <= k - 4 < TILES:
                    low_xn2(k - 4)

            def te(ap):
                return ap.rearrange("p (t e) -> p t e", e=EXPERTS)

            def per_tile(ap):
                return bc(ap.unsqueeze(2), [P, TILES, EXPERTS])

            logits = te(final_bank[0][:, 0:TE])
            rank = bc(C("rank").unsqueeze(1), [P, TILES, EXPERTS])
            top, g1, g2, tot, w_ = (r_s[:, j, :] for j in range(5))
            dve.wait_ge(logits_done, 1)
            link(nc.vector.tensor_reduce(top, logits, AX.X, ALU.max))
            nc.vector.tensor_tensor(te(r_l[:]), logits, per_tile(top), ALU.subtract)\
                .then_inc(logits_shifted, 1)
            dve.wait_ge(gates_exp, 1)
            link(nc.vector.tensor_reduce(tot, te(r_e[:]), AX.X, ALU.add))
            link(nc.vector.reciprocal(tot, tot))
            link(nc.vector.tensor_tensor(te(r_g[:]), te(r_e[:]), per_tile(tot), ALU.mult))
            link(nc.vector.tensor_reduce(g1, te(r_g[:]), AX.X, ALU.max))
            link(nc.vector.tensor_tensor(te(r_a[:]), te(r_g[:]), per_tile(g1), ALU.is_equal))
            link(nc.vector.tensor_tensor(te(r_a[:]), te(r_a[:]), rank, ALU.mult))
            link(nc.vector.tensor_reduce(top, te(r_a[:]), AX.X, ALU.max))
            link(nc.vector.tensor_tensor(te(r_m[:, 0, :]), te(r_a[:]), per_tile(top), ALU.is_equal))
            link(nc.vector.scalar_tensor_tensor(out=r_b[:], in0=r_m[:, 0, :], scalar=-BIG,
                                                in1=final_bank[0][:, 0:TE], op0=ALU.mult, op1=ALU.add))
            link(nc.vector.tensor_reduce(top, te(r_b[:]), AX.X, ALU.max))
            link(nc.vector.tensor_tensor(te(r_a[:]), te(r_b[:]), per_tile(top), ALU.is_equal))
            link(nc.vector.tensor_tensor(te(r_a[:]), te(r_a[:]), rank, ALU.mult))
            link(nc.vector.tensor_reduce(top, te(r_a[:]), AX.X, ALU.max))
            link(nc.vector.tensor_tensor(te(r_m[:, 1, :]), te(r_a[:]), per_tile(top), ALU.is_equal))
            link(nc.vector.tensor_copy(r_mb[:], r_m[:]))
            nc.vector.memset(r_before[:, :, 0, :], 0.0).then_inc(before_zero, 1)
            dve.wait_ge(before_zero, 1)
            mb = r_mb[:].rearrange("p c (t e) -> p c t e", e=EXPERTS)
            for j in range(1, TILES):
                link(nc.vector.tensor_tensor(r_before[:, :, j, :], r_before[:, :, j - 1, :],
                                             mb[:, :, j - 1, :], ALU.add))
            link(nc.vector.tensor_tensor(r_s[:, 5, :], r_before[:, 0, TILES - 1, :],
                                         mb[:, 0, TILES - 1, :], ALU.add))
            nc.vector.tensor_tensor(r_before[:, 1], r_before[:, 1],
                                    bc(r_s[:, 5, :].unsqueeze(1), [P, TILES, EXPERTS]), ALU.add)\
                .then_inc(masks_done, 1)
            link(nc.vector.tensor_tensor(r_a[:], r_g[:], r_m[:, 1, :], ALU.mult))
            link(nc.vector.tensor_reduce(g2, te(r_a[:]), AX.X, ALU.add))
            link(nc.vector.tensor_tensor(w_, g1, g2, ALU.add))
            link(nc.vector.tensor_scalar(w_, w_, 1e-9, None, ALU.add))
            link(nc.vector.reciprocal(w_, w_))
            link(nc.vector.tensor_tensor(r_w[:, 0, :], g1, w_, ALU.mult))
            link(nc.vector.tensor_tensor(r_w[:, 1, :], g2, w_, ALU.mult))
            dve.wait_ge(ranked, 1)
            link(nc.vector.tensor_tensor(r_pm[:].rearrange("p c n -> p (c n)"), final_bank[1][:, 0:2 * TE],
                                         r_m[:].rearrange("p c n -> p (c n)"), ALU.mult))
            link(nc.vector.tensor_reduce(r_pos[:], r_pm[:].rearrange("p c (t e) -> p c t e", e=EXPERTS),
                                         AX.X, ALU.add))
            link(nc.vector.tensor_scalar(r_pos[:], r_pos[:], float(CAPACITY), None, ALU.is_lt))
            link(nc.vector.tensor_tensor(r_w[:], r_w[:], r_pos[:], ALU.mult))
            link(nc.vector.tensor_tensor(r_wm[:].rearrange("p c (t e) -> p c t e", e=EXPERTS),
                                         r_m[:].rearrange("p c (t e) -> p c t e", e=EXPERTS),
                                         bc(r_w[:].unsqueeze(3), [P, 2, TILES, EXPERTS]), ALU.mult))
            nc.vector.tensor_tensor(gate[:], r_wm[:, 0, :], r_wm[:, 1, :], ALU.add).then_inc(gate_done, 1)

            def low(n, r):
                dve.wait_ge(h_hi_done, n + 1)
                nc.vector.tensor_tensor(h_lo[:, r, :], hidden_bank[r][:], h_hi[:, r, :].bitcast(f32),
                                        ALU.subtract).then_inc(h_done, 1)

            def gated(m, e, s, first):
                dve.wait_ge(down_done, m * HCH + HCH)
                if not first:
                    dve.wait_ge(y_added, m - 1)
                nc.vector.tensor_tensor(
                    y_gated[:, s, :], y_bank[s][:],
                    gate_all[:, :, :].rearrange("p e t -> p (e t)")[:, bass.ds(e * TOKENS + s * 512, 512)],
                    ALU.mult).then_inc(y_gated_done, 1)

            def pair(i, first):
                for j in range(2 * STEPS):
                    low(i * (2 * STEPS) + j, j % RING)
                    if j % HCH == 1 and not (first and j < HCH):
                        m = j // HCH - 1
                        gated(i * 4 + m, i * 2 + m // 2 if m >= 0 else i * 2 - 1, m % 2, first and m < 2)

            low(0, 0)
            low(1, 1)
            low(2, 2)
            low(3, 3)
            dve.wait_ge(gate_spread, 16 * EXPERTS)
            for j in range(HCH, 2 * STEPS):
                low(j, j % RING)
                if j % HCH == 1:
                    m = j // HCH - 1
                    gated(m, m // 2, m % 2, m < 2)
            with dve.Fori(1, EXPERTS // 2) as i:
                pair(i, False)
            gated(2 * EXPERTS - 1, EXPERTS - 1, 1, False)
            for t in range(TILES):
                dve.wait_ge(final_done, t + 1)
                nc.vector.tensor_tensor(result[:, t, :], final_bank[t % 2][:, 0:P], X1[:, t, :], ALU.add)\
                    .then_inc(result_done, 1)

        @block.tensor
        def _(pe):
            mm, turn = nc.tensor.matmul, nc.tensor.transpose
            ident = C("ident")

            pe.wait_ge(ld_pa, 16)
            mm(bank[6][:, 0:BATCH * KEYS], A("wk"), A("ctx"), start=True, stop=True)\
                .then_inc(keys_projected, 1)
            for b in range(BATCH):
                pe.wait_ge(ctx_copied, b + 1)
                for c in range(CHUNKS):
                    rows = P if c < CHUNKS - 1 else LAST_ROWS
                    o = (b * CHUNKS + c) * SPAN * HEAD_DIM
                    h = FIRST_HEAD[c] * HEAD_DIM
                    last = mm(bank[7][0:rows, o:o + SPAN * HEAD_DIM], ctx_rep[:, b, c * P:c * P + rows],
                              A("wv")[:, h:h + SPAN * HEAD_DIM], start=True, stop=True)
            last.then_inc(values_projected, 1)
            pe.wait_ge(ld_cst, 16)
            pe.wait_ge(ld_pb, 16)
            for s in range(2):
                for t in range(s * HT, (s + 1) * HT):
                    pe.wait_ge(normed, t + 1)
                    last = turn(bank[3 + s][:, (t % HT) * P:(t % HT + 1) * P], xn[:, t, :], ident)
                last.then_inc(norm_turned, 1)
            for s in range(2):
                pe.wait_ge(norm_copied, s + 1)
                mm(bank[s][:], B("wq"), xnT[:, s * 512:(s + 1) * 512], start=True, stop=True)\
                    .then_inc(q_projected, 1)

            def three(o, w_hi, w_lo, m_hi, m_lo, start, stop):
                mm(o, w_lo, m_hi, start=start, stop=False)
                mm(o, w_hi, m_lo, start=False, stop=False)
                return mm(o, w_hi, m_hi, start=False, stop=stop)

            def scores(t):
                b = t // TILES_PER_BATCH
                tt = slice(t * P, (t + 1) * P)
                for g, (h0, h1) in enumerate(GROUPS):
                    if t >= 1:
                        pe.wait_ge(shift_done, 3 * (t - 1) + g + 1)
                    cc = slice(h0 * KEYS, h1 * KEYS)
                    three(score_bank[g][:, 0:(h1 - h0) * KEYS], q_hi[:, tt], q_lo[:, tt],
                          kb_hi[:, b, cc], kb_lo[:, b, cc], True, True).then_inc(scored, 1)

            def turns(t):
                for j, (c0, c1) in enumerate(QUADS):
                    u = 3 * t + j
                    need = min(g for g, (_, h1) in enumerate(GROUPS) if h1 * KEYS >= min(c1 * P, FLAT))
                    pe.wait_ge(shift_done, 3 * t + need + 1)
                    if u >= 2:
                        pe.wait_ge(exp_done, u - 1)
                    for c in range(c0, c1):
                        last = turn(turned_bank[u % 2][:, (c - c0) * P:(c - c0 + 1) * P],
                                    shifted[:, t % 2, c * P:(c + 1) * P], ident)
                    last.then_inc(turned, 1)

            def weigh(t):
                b = t // TILES_PER_BATCH
                if t >= 1:
                    pe.wait_ge(attn_done, t)
                for j, (c0, c1) in enumerate(QUADS):
                    pe.wait_ge(exp_done, 3 * t + j + 1)
                    for c in range(c0, c1):
                        rows = P if c < CHUNKS - 1 else LAST_ROWS
                        w = probs[0:rows, t % 2, c * P:(c + 1) * P]
                        if c == 0:
                            mm(out_bank[:, 0:HEADS * VW], w, v_first[:, b, :], start=True, stop=False)
                        else:
                            o = FIRST_HEAD[c] * VW
                            last = mm(out_bank[:, o:o + SPAN * VW], w, v_rest[0:rows, b, c, :],
                                      start=False, stop=(c == CHUNKS - 1))
                last.then_inc(weighted, 1)

            def turn_attn(t):
                pe.wait_ge(attn_done, t + 1)
                if t >= 1:
                    pe.wait_ge(x1_done, t)
                turn(proj_bank[:, 0:P], attn[:, t % 2, :], ident).then_inc(attn_turned, 1)

            def project(t):
                pe.wait_ge(attn_copied, t + 1)
                mm(proj_bank[:, 0:P], attnT[:, t % 2, :], B("wo"), start=True, stop=True)\
                    .then_inc(projected, 1)

            def turn_xn2(t):
                pe.wait_ge(xn2_done, t + 1)
                if t >= 1:
                    pe.wait_ge(x2_done, t)
                turn(xn2_bank[:, 0:P], xn2[:, t % 2, :], ident).then_inc(xn2_turned, 1)

            pe.wait_ge(kb_done, 2 * HEADS)
            pe.wait_ge(q_done, 2)
            for k in range(TILES + 4):
                if 0 <= k - 3 < TILES:
                    turn_attn(k - 3)
                if k < TILES:
                    scores(k)
                if 0 <= k - 3 < TILES:
                    project(k - 3)
                if 0 <= k - 1 < TILES:
                    turns(k - 1)
                if 0 <= k - 2 < TILES:
                    if k == 2:
                        pe.wait_ge(values_set, 3 * BATCH + 1)
                    weigh(k - 2)
                if 0 <= k - 4 < TILES:
                    turn_xn2(k - 4)

            pe.wait_ge(x2_done, TILES)
            pe.wait_ge(wg_done, 1)
            for t in range(TILES):
                tt = slice(t * P, (t + 1) * P)
                last = three(final_bank[0][:, t * EXPERTS:(t + 1) * EXPERTS], x2_hi[:, tt], x2_lo[:, tt],
                             wg_hi[:], wg_lo[:], True, True)
            last.then_inc(logits_done, 1)

            def up(n, u, s, c, r, first):
                if not first:
                    pe.wait_ge(h_done, n - (RING - 1))
                cc = slice(c * P, (c + 1) * P)
                ss = slice(s * 512, (s + 1) * 512)
                three(hidden_bank[r][:], w1_hi[:, u, cc], w1_lo[:, u, cc], x2_hi[:, ss], x2_lo[:, ss],
                      True, True).then_inc(up_done, 1)

            def down(n, m, u, s, c, r, first):
                pe.wait_ge(h_done, n + 1)
                if c == 0 and not first:
                    pe.wait_ge(y_gated_done, m - 1)
                cc = slice(c * P, (c + 1) * P)
                last = three(y_bank[s][:], w2_hi[:, u, cc], w2_lo[:, u, cc], h_hi[:, r, :], h_lo[:, r, :],
                             c == 0, c == HCH - 1)
                last.then_inc(down_done, 1)

            AHEAD = 3

            def step_up(i, j, first):
                u, s, c = j // STEPS % 2, j // HCH % HALVES, j % HCH
                if j % STEPS == 0:
                    pe.wait_ge(w1_split, i * 2 + (j // STEPS + 1))
                up(i * (2 * STEPS) + j, u, s, c, j % RING, first)

            def rank_choices():
                pe.wait_ge(masks_done, 1)
                pe.wait_ge(upper_set, 1)
                pe.wait_ge(consts_set, 3)
                o = final_bank[1][:, 0:2 * TE]
                mm(o, upper_bf[:], r_mb[:].rearrange("p c n -> p (c n)"), start=True, stop=False)
                mm(o, ones_bf[:], r_before[:].rearrange("p c t e -> p (c t e)"), start=False, stop=True)\
                    .then_inc(ranked, 1)

            def turn_gates():
                pe.wait_ge(gate_done, 1)
                for t in range(TILES):
                    last = turn(final_bank[t // HT][0:EXPERTS, (t % HT) * P:(t % HT + 1) * P],
                                gate[:, t * EXPERTS:(t + 1) * EXPERTS], ident)
                    if t % HT == HT - 1:
                        last.then_inc(gate_turned, 1)

            rank_choices()
            turn_gates()
            for j in range(AHEAD):
                step_up(0, j, True)

            def run_pair(i, first, last):
                for j in range(2 * STEPS):
                    if j + AHEAD < 2 * STEPS or not last:
                        step_up(i, j + AHEAD, first and j + AHEAD < RING)
                    if j % STEPS == 0:
                        pe.wait_ge(w2_split, i * 2 + (j // STEPS + 1))
                    down(i * (2 * STEPS) + j, i * 4 + j // HCH, j // STEPS, j // HCH % HALVES, j % HCH,
                         j % RING, first and j < 2 * HCH)

            run_pair(0, True, False)
            with pe.Fori(1, EXPERTS // 2 - 1) as i:
                run_pair(i, False, False)
            run_pair(EXPERTS // 2 - 1, False, True)

            pe.wait_ge(ld_b2, 16)
            pe.wait_ge(gateT_done, 2)
            for t in range(TILES):
                pe.wait_ge(y_added, 2 * EXPERTS - 1 + t // HT)
                if t >= 2:
                    pe.wait_ge(result_done, t - 1)
                tt = slice(t * P, (t + 1) * P)
                mm(final_bank[t % 2][:, 0:P], gateT[:, tt], b2_sb[:], start=True, stop=False)
                mm(final_bank[t % 2][:, 0:P], y_sum[:, tt], ident, start=False, stop=True)\
                    .then_inc(final_done, 1)


def constants():
    import numpy as np
    ident = np.eye(P)
    head = np.arange(P)[:, None] // HEAD_DIM == np.arange(HEADS)[None, :]
    flat = np.arange(CHUNKS)[None, :, None] * P + np.arange(P)[:, None, None]
    of = np.array(FIRST_HEAD)[None, :, None] + np.arange(SPAN)[None, None, :]
    vmask = (flat // KEYS == of).reshape(P, CHUNKS * SPAN)
    upper = np.arange(P)[:, None] < np.arange(P)[None, :]
    rank = np.broadcast_to(EXPERTS - np.arange(EXPERTS), (P, EXPERTS))
    return np.concatenate([ident, head, vmask, upper, rank], axis=1).astype(np.float32)


def kernel(x, ctx_1024, mask_BxSxS2_if1, L0_xattn_Wq, L0_xattn_bq, L0_xattn_Wk, L0_xattn_bk,
           L0_xattn_Wv, L0_xattn_bv, L0_xattn_Wo, L0_xattn_bo, L0_ffn_Wg, L0_ffn_W1, L0_ffn_b1,
           L0_ffn_W2, L0_ffn_b2):
    import numpy as np
    import concourse.bacc as bacc
    from concourse.bass_utils import run_bass_kernel_spmd

    a = np.asarray
    ctx_t = a(ctx_1024).reshape(BATCH * KEYS, EMB).T
    par_a = np.concatenate([a(L0_xattn_Wk).T, ctx_t, a(L0_xattn_Wv).T, a(L0_xattn_bk)[:, None],
                            a(L0_xattn_bq)[:, None]], axis=1)
    par_b = np.concatenate([a(L0_xattn_Wq).T, a(L0_xattn_Wo).T, a(L0_ffn_Wg),
                            a(L0_ffn_b1).reshape(EXPERTS * HCH, P).T], axis=1)
    bias_v = np.concatenate([a(L0_xattn_bv)[h * HEAD_DIM:(h + SPAN) * HEAD_DIM] for h in FIRST_HEAD])
    arrays = {
        "x": a(x).reshape(TOKENS, EMB), "par_a": par_a, "par_b": par_b, "bias_v": bias_v,
        "bias_o": a(L0_xattn_bo), "w1": a(L0_ffn_W1), "w2": a(L0_ffn_W2), "b2": a(L0_ffn_b2),
        "const": constants(),
    }
    arrays = {f"in_{k}": np.ascontiguousarray(v) for k, v in arrays.items()}
    nc = bacc.Bacc("TRN2", target_bir_lowering=False, num_devices=1)
    args = [nc.dram_tensor(k, v.shape, mybir.dt.from_np(v.dtype), kind="ExternalInput").ap()
            for k, v in arrays.items()]
    args.append(nc.dram_tensor("out_0", (TOKENS, EMB), mybir.dt.float32, kind="ExternalOutput").ap())
    xattn_moe(nc, *args)
    r = run_bass_kernel_spmd(nc, [arrays], core_ids=[0])
    return r.results[0]["out_0"].reshape(BATCH, SEQ, EMB)
```

```python
import concourse.bass as bass
from concourse import mybir
from contextlib import ExitStack


BATCH, SEQ, EMB = 2, 512, 128
KEYS = 77
HEADS = 16
HEAD_DIM = EMB // HEADS
EXPERTS = 8
HIDDEN = 512
TOP_K = 2
TOKENS = BATCH * SEQ
CAPACITY = 2 * TOP_K * TOKENS // EXPERTS
P = 128
TILES = TOKENS // P
BATCH_TILES = SEQ // P
HALF = 512
HALVES = TOKENS // HALF
HT = HALF // P

GH = 32 // HEAD_DIM
GROUPS = HEADS // GH
GCOLS = GH * KEYS
GCHUNKS = -(-GCOLS // P)
GWIDTH = GCHUNKS * P
CHUNKS = GROUPS * GCHUNKS
WIDTH = CHUNKS * P
QUAD = 4
QUADS = CHUNKS // QUAD

HCH = HIDDEN // P
STEPS = HALVES * HCH
RING = 4
AHEAD = 3
PAIR = 2 * STEPS
LN_EPS = 1e-5
GATE_EPS = 1e-9
BIG = 3.0e38
TE = TILES * EXPERTS

PAR_A = [("wk", EMB), ("ctx", BATCH * KEYS), ("wv", EMB), ("bk", 1), ("bq", 1)]
PAR_B = [("wq", EMB), ("wo", EMB), ("wg", EXPERTS), ("b1", EXPERTS * HCH)]
CONST = [("ident", P), ("head", GH), ("vmask", CHUNKS * GH), ("upper", P), ("rank", EXPERTS)]


def columns(parts):
    at, out = 0, {}
    for name, width in parts:
        out[name] = (at, at + width)
        at += width
    return out, at


def xattn_moe(nc, x, par_a, par_b, bias_v, bias_o, w1, w2, b2, const, out):
    f32, f32r, bf16 = mybir.dt.float32, mybir.dt.float32r, mybir.dt.bfloat16
    ALU, ACT, AX = mybir.AluOpType, mybir.ActivationFunctionType, mybir.AxisListType
    SCALE = float(HEAD_DIM) ** -0.5
    col_a, width_a = columns(PAR_A)
    col_b, width_b = columns(PAR_B)
    col_c, width_c = columns(CONST)

    ctx = ExitStack()
    with ctx:
        def sb(name, shape, dt=f32):
            return ctx.enter_context(nc.sbuf_tensor(name, shape, dt))

        def sems(names):
            return [ctx.enter_context(nc.semaphore(n)) for n in names.split()]

        pa = sb("pa", [P, width_a])
        pb = sb("pb", [P, width_b])
        cst = sb("cst", [P, width_c])

        def A(name):
            return pa[:, col_a[name][0]:col_a[name][1]]

        def B(name):
            return pb[:, col_b[name][0]:col_b[name][1]]

        def C(name):
            return cst[:, col_c[name][0]:col_c[name][1]]

        X = sb("X", [P, TILES, EMB])
        bv_all = sb("bv_all", [P, CHUNKS * 32])
        bo_all = sb("bo_all", [P, EMB])
        b2_diag = sb("b2_diag", [TE, TILES, EMB])
        neg_half = sb("neg_half", [P, TILES])
        Xb = sb("Xb", [P, TILES, EMB])
        X1 = sb("X1", [P, TILES, EMB])
        stats = sb("stats", [P, TILES, 6])
        mv = sb("mv", [P, TILES, 2])
        rstd = sb("rstd", [P, TILES])
        xn = sb("xn", [P, TILES, EMB])
        xnT = sb("xnT", [P, TOKENS])
        q_hi = sb("q_hi", [P, TOKENS], f32r)
        q_lo = sb("q_lo", [P, TOKENS], f32r)
        kt_hi = sb("kt_hi", [P, BATCH, KEYS], f32r)
        kt_lo = sb("kt_lo", [P, BATCH, KEYS], f32r)
        kb_hi = sb("kb_hi", [P, BATCH, GCOLS], f32r)
        kb_lo = sb("kb_lo", [P, BATCH, GCOLS], f32r)
        ctx_rep = sb("ctx_rep", [P, BATCH, WIDTH])
        v_sum = sb("v_sum", [P, CHUNKS * 32])
        v_blk = sb("v_blk", [P, BATCH, CHUNKS, 32])
        v_ones = sb("v_ones", [P, CHUNKS, 32])
        mx = sb("mx", [P, 2, HEADS])
        shifted = sb("shifted", [P, 2, WIDTH])
        probs = sb("probs", [P, 2, WIDTH])
        rec = sb("rec", [P, 2, P])
        attnT = sb("attnT", [P, 2, P])
        stats2 = sb("stats2", [P, 2, 6])
        mv2 = sb("mv2", [P, 2, 2])
        ln2 = sb("ln2", [P, 2, 3])
        xn2 = sb("xn2", [P, 2, EMB])
        x2_hi = sb("x2_hi", [P, TOKENS], f32r)
        x2_lo = sb("x2_lo", [P, TOKENS], f32r)
        wg_hi = sb("wg_hi", [P, EXPERTS], f32r)
        wg_lo = sb("wg_lo", [P, EXPERTS], f32r)
        warm = sb("warm", [P, 512], bf16)
        table = sb("table", [P, 1])
        ones_bf = sb("ones_bf", [P, P], bf16)
        upper_bf = sb("upper_bf", [P, P], bf16)
        r_l = sb("r_l", [P, TE])
        r_e = sb("r_e", [P, TE])
        r_a = sb("r_a", [P, TE])
        r_b = sb("r_b", [P, TE])
        r_c = sb("r_c", [P, TE])
        r_m = sb("r_m", [P, 2, TE], bf16)
        r_top = sb("r_top", [P, 6, TILES])
        r_g = sb("r_g", [P, 2, TILES])
        r_pm = sb("r_pm", [P, 2, TE])
        r_pos = sb("r_pos", [P, 2, TILES])
        r_wm = sb("r_wm", [P, 2, TE])
        gate = sb("gate", [P, TE])
        gateT = sb("gateT", [TE, P])
        gate_all = sb("gate_all", [P, EXPERTS, TOKENS])
        w1_raw = sb("w1_raw", [P, 2, HIDDEN])
        w2_raw = sb("w2_raw", [P, 2, HCH * EMB])
        w1_hi = sb("w1_hi", [P, 2, HIDDEN], f32r)
        w1_lo = sb("w1_lo", [P, 2, HIDDEN], f32r)
        w2_hi = sb("w2_hi", [P, 2, HCH * EMB], f32r)
        w2_lo = sb("w2_lo", [P, 2, HCH * EMB], f32r)
        b1_pair = sb("b1_pair", [P, 2 * HCH])
        h_hi = sb("h_hi", [P, RING, HALF], f32r)
        h_lo = sb("h_lo", [P, RING, HALF], f32r)
        y_stash = sb("y_stash", [P, 2 * HALVES, HALF])
        y_gated = sb("y_gated", [P, HALVES, HALF])
        y_sum = sb("y_sum", [P, TOKENS])
        result = sb("result", [P, TILES, EMB])

        score = ctx.enter_context(nc.psum_tensor("score", [P, GROUPS, 512], f32))
        bank = {i: ctx.enter_context(nc.psum_tensor(f"bank{i}", [P, 512], f32)) for i in range(4, 8)}
        turned_bank = [bank[4], bank[5]]
        out_bank, mixed_bank = bank[6], bank[7]
        y_bank = [bank[4], bank[5]]
        final_bank = [bank[6], bank[7]]
        turned_x2 = mixed_bank[:, 0:P]
        logits = mixed_bank[:, P:P + TE]
        projection = out_bank[:, 2 * P:3 * P]
        place = out_bank[:, 0:2 * TE]
        gate_turn = out_bank[0:TE, 2 * P:3 * P]

        ld_pa, ld_pb, ld_cst, ld_x0, ld_x1, ld_bv, ld_bo, ld_b2 = sems(
            "ld_pa ld_pb ld_cst ld_x0 ld_x1 ld_bv ld_bo ld_b2")
        pool_chain, dve_chain, consts_set, zeros_set, v_ones_set, warm_set, table_loaded = sems(
            "pool_chain dve_chain consts_set zeros_set v_ones_set warm_set table_loaded")
        keys_projected, kt_hi_done, kt_done, kb_hi_done, kb_lo_done = sems(
            "keys_projected kt_hi_done kt_done kb_hi_done kb_lo_done")
        ctx_copied, values_projected, v_sum_done, values_set = sems(
            "ctx_copied values_projected v_sum_done values_set")
        stats_done, moments_done, rstd_done, normed, norm_turned, norm_copied = sems(
            "stats_done moments_done rstd_done normed norm_turned norm_copied")
        q_projected, q_hi_done, q_done, bo_added, upper_set, wg_done = sems(
            "q_projected q_hi_done q_done bo_added upper_set wg_done")
        scored, max_done, shift_done, turned, exp_done = sems(
            "scored max_done shift_done turned exp_done")
        weighted, rec_done, attn_done, projected, x1_done = sems(
            "weighted rec_done attn_done projected x1_done")
        stats2_done, moments2_done, xn2_done, xn2_turned, x2_hi_done, x2_done = sems(
            "stats2_done moments2_done xn2_done xn2_turned x2_hi_done x2_done")
        logits_done, logits_shifted, tanh_done, root_done, squared, masks_done, placed, gate_done = sems(
            "logits_done logits_shifted tanh_done root_done squared masks_done placed gate_done")
        gate_turned, gateT_done, gate_stored = sems("gate_turned gateT_done gate_stored")
        gate_spread = sems(" ".join(f"gate_spread{i}" for i in range(EXPERTS)))
        w1_loaded = sems("w1_loaded0 w1_loaded1")
        w2_loaded = sems("w2_loaded0 w2_loaded1")
        slot_ready, w_hi_done, w1_split, w2_split = sems("slot_ready w_hi_done w1_split w2_split")
        b1_here, up_done, gelu_done, h_hi_done, h_done, down_done = sems(
            "b1_here up_done gelu_done h_hi_done h_done down_done")
        y_stashed, stash_gated, stash_added, y_gated_done, y_added = sems(
            "y_stashed stash_gated stash_added y_gated_done y_added")
        final_done, result_done, stored = sems("final_done result_done stored")

        gate_rows = nc.dram_tensor("gate_rows", (EXPERTS, TOKENS), f32, kind="Internal").ap()
        x_v = x.rearrange("(t p) e -> p t e", p=P)
        out_v = out.rearrange("(t p) e -> p t e", p=P)
        w1_v = w1.rearrange("e d f -> d e f")
        w2_v = w2.rearrange("e (c p) d -> p e c d", p=P)

        SHIFT_AT, FIRST_AT, SECOND_AT, ROOT_AT, GATES_AT, WEIGHTS_AT, DROP_AT = 1, 2, 3, 4, 6, 7, 8
        TANH_AT, SQUARE_AT, GATE_COPY_AT, GATE_STORE_AT = 3, 6, 12, 15
        PLACE_AT, TURN_AT = 4, 9
        WARM_UP = 7
        DRAIN_UP = {TILES: (0, 1), TILES + 1: (2, 3)}
        DRAIN_HIDDEN = {TILES + 1: (0,), TILES + 2: (1, 2)}
        DRAIN_LOW = {TILES + 2: (0,), TILES + 3: (1,)}
        DRAIN_DOWN = {TILES + 2: (0,), TILES + 3: (1,)}

        Q_PIECES = [(0, P), (P, HALF), (HALF, TOKENS)]

        def norm_piece(n):
            a, b = Q_PIECES[n]
            return (bank[4], bank[5], mixed_bank)[n][:, 0:b - a]

        def q_piece(n):
            a, b = Q_PIECES[n]
            return (out_bank, bank[4], mixed_bank)[n][:, 0:b - a]

        values_bank = mixed_bank[:, 0:CHUNKS * 32]

        block = ctx.enter_context(nc.Block())

        @block.sync
        def _(sp):
            sp.dma_start(X[:, 0:HT, :], x_v[:, 0:HT, :]).then_inc(ld_x0, 16)
            sp.dma_start(cst[:], const).then_inc(ld_cst, 16)
            sp.dma_start(X[:, HT:TILES, :], x_v[:, HT:TILES, :]).then_inc(ld_x1, 16)

            def load_expert(e, u):
                sp.dma_start(w1_raw[:, u, :], w1_v[:, bass.ds(e, 1), :].rearrange("p a f -> p (a f)"))\
                    .then_inc(w1_loaded[u], 16)
                sp.dma_start(w2_raw[:, u, :].rearrange("p (c d) -> p c d", c=HCH),
                             w2_v[:, bass.ds(e, 1), :, :].rearrange("p a c d -> p (a c) d"))\
                    .then_inc(w2_loaded[u], 16)

            sp.dma_start(bv_all[:], bias_v.partition_broadcast(P)).then_inc(ld_bv, 16)
            sp.dma_start(bo_all[:], bias_o.partition_broadcast(P)).then_inc(ld_bo, 16)
            for e in range(2):
                load_expert(e, e)
            sp.dma_start(b2_diag[:], b2).then_inc(ld_b2, 16)
            for e in range(2, 4):
                sp.wait_ge(w1_split, e - 1)
                sp.wait_ge(w2_split, e - 1)
                load_expert(e, e % 2)
            with sp.Fori(2, EXPERTS // 2) as i:
                for u in range(2):
                    sp.wait_ge(w1_split, i * 2 + (u - 1))
                    sp.wait_ge(w2_split, i * 2 + (u - 1))
                    load_expert(i * 2 + u, u)
            for s in range(HALVES):
                sp.wait_ge(result_done, s + 1)
                sp.dma_start(out_v[:, s * HT:(s + 1) * HT, :],
                             result[:, s * HT:(s + 1) * HT, :]).then_inc(stored, 16)
            sp.wait_ge(stored, 16 * HALVES)

        @block.gpsimd
        def _(pool):
            chain = [0]

            def link(ins):
                chain[0] += 1
                ins.then_inc(pool_chain, 1)
                pool.wait_ge(pool_chain, chain[0])

            nc.gpsimd.memset(neg_half[:], -0.5).then_inc(consts_set, 1)
            for padded in (ctx_rep, shifted):
                nc.gpsimd.memset(padded[:].rearrange("p b (g w) -> p (b g) w", w=GWIDTH)[:, :, GCOLS:], 0.0)\
                    .then_inc(zeros_set, 1)
            nc.gpsimd.memset(ones_bf[:], 1.0).then_inc(consts_set, 1)

            pool.wait_ge(consts_set, 1)

            def root(s):
                pool.wait_ge(moments_done, HT * (s + 1))
                sl = slice(s * HT, (s + 1) * HT)
                link(nc.gpsimd.tensor_scalar(rstd[:, sl], mv[:, sl, 1], LN_EPS, None, ALU.add))
                nc.gpsimd.tensor_tensor(rstd[:, sl], rstd[:, sl], neg_half[:, sl], ALU.pow)\
                    .then_inc(rstd_done, 1)

            def low_keys(b):
                for j in range(GH):
                    nc.gpsimd.tensor_scalar(kb_lo[:, b, j * KEYS:(j + 1) * KEYS], kt_lo[:, b, :].bitcast(f32),
                                            C("head")[:, j:j + 1], 1.0, ALU.mult, ALU.mult)\
                        .then_inc(kb_lo_done, 1)

            root(0)
            pool.wait_ge(ld_cst, 16)
            pool.wait_ge(kt_done, 1)
            low_keys(0)
            root(1)
            low_keys(1)
            vm = C("vmask").rearrange("p (n j) -> p n j", n=CHUNKS)
            nc.gpsimd.tensor_copy(v_ones[:].rearrange("p n (j d) -> p n j d", j=GH),
                                  vm.unsqueeze(3).broadcast_to([P, CHUNKS, GH, HEAD_DIM])).then_inc(v_ones_set, 1)
            pool.wait_ge(ld_bo, 16)
            pool.wait_ge(ld_x0, 16)
            pool.wait_ge(ld_x1, 16)
            for s in range(HALVES):
                sl = slice(s * HT, (s + 1) * HT)
                nc.gpsimd.tensor_tensor(Xb[:, sl, :], X[:, sl, :],
                                        bo_all[:].unsqueeze(1).broadcast_to([P, HT, EMB]), ALU.add)\
                    .then_inc(bo_added, 1)
            pool.wait_ge(ld_pb, 16)
            link(nc.gpsimd.tensor_copy(wg_hi[:], B("wg")))
            nc.gpsimd.tensor_tensor(wg_lo[:], B("wg"), wg_hi[:].bitcast(f32), ALU.subtract)\
                .then_inc(wg_done, 1)

            def split(n, u, raw, hi, lo, loaded, level, signal):
                pool.wait_ge(loaded[u], level)
                pool.sem_inc(slot_ready, 1)
                nc.gpsimd.tensor_scalar(hi[:, u, :], raw[:, u, :], 1.0, 1.0, ALU.mult, ALU.mult)\
                    .then_inc(w_hi_done, 1)
                pool.wait_ge(w_hi_done, n)
                nc.gpsimd.tensor_tensor(lo[:, u, :], raw[:, u, :], hi[:, u, :].bitcast(f32),
                                        ALU.subtract).then_inc(signal, 1)

            def norm2(t):
                p = t % 2
                pool.wait_ge(moments2_done, t + 1)
                nc.gpsimd.tensor_scalar(ln2[:, p, 0:1], mv2[:, p, 1:2], LN_EPS, None, ALU.add)\
                    .then_inc(pool_chain, 1)
                nc.gpsimd.tensor_scalar(ln2[:, p, 1:2], mv2[:, p, 0:1], -1.0, None, ALU.mult)\
                    .then_inc(pool_chain, 1)
                pool.wait_ge(pool_chain, chain[0] + 1)
                chain[0] += 2
                link(nc.gpsimd.tensor_tensor(ln2[:, p, 2:3], ln2[:, p, 0:1], neg_half[:, 0:1], ALU.pow))
                if t >= 2:
                    pool.wait_ge(xn2_turned, t - 1)
                nc.gpsimd.tensor_scalar(xn2[:, p, :], X1[:, t, :], ln2[:, p, 1:2], ln2[:, p, 2:3],
                                        ALU.add, ALU.mult).then_inc(xn2_done, 1)

            split(1, 0, w1_raw, w1_hi, w1_lo, w1_loaded, 16, w1_split)
            split(2, 0, w2_raw, w2_hi, w2_lo, w2_loaded, 16, w2_split)
            norm2(0)
            split(3, 1, w1_raw, w1_hi, w1_lo, w1_loaded, 16, w1_split)
            norm2(1)
            split(4, 1, w2_raw, w2_hi, w2_lo, w2_loaded, 16, w2_split)
            for t in range(2, TILES):
                norm2(t)
            nc.gpsimd.memset(y_sum[:], 0.0).then_inc(zeros_set, 1)
            pool.wait_ge(zeros_set, 3)

            def add_up(m, s):
                pool.wait_ge(y_gated_done, m + (1 - 2 * HALVES))
                half = y_sum[:, s * HALF:(s + 1) * HALF]
                nc.gpsimd.tensor_tensor(half, half, y_gated[:, s, :], ALU.add).then_inc(y_added, 1)

            def split_next(i, u):
                pool.wait_ge(up_done, i * PAIR + STEPS * (u + 1))
                split(i * 4 + (5 + 2 * u), u, w1_raw, w1_hi, w1_lo, w1_loaded, i * 16 + 32, w1_split)
                pool.wait_ge(down_done, i * PAIR + STEPS * (u + 1))
                split(i * 4 + (6 + 2 * u), u, w2_raw, w2_hi, w2_lo, w2_loaded, i * 16 + 32, w2_split)

            for u in range(2):
                split_next(0, u)
            with pool.Fori(1, EXPERTS // 2 - 1) as i:
                for u in range(2):
                    for s in range(HALVES):
                        add_up(i * 4 + (2 * u + s), s)
                    split_next(i, u)
            last = 2 * EXPERTS - 2 * HALVES
            for m in range(2 * HALVES):
                s = m % HALVES
                pool.wait_ge(y_stashed, m + 1)
                if s == 0:
                    pool.wait_ge(gate_spread[m // HALVES], 16)
                nc.gpsimd.tensor_tensor(y_stash[:, m, :], y_stash[:, m, :],
                                        gate_all[:, m // HALVES, s * HALF:(s + 1) * HALF], ALU.mult)\
                    .then_inc(stash_gated, 1)
                pool.wait_ge(stash_gated, m + 1)
                if m < HALVES:
                    pool.wait_ge(y_added, last - 3 * HALVES + m + 1)
                else:
                    pool.wait_ge(stash_added, m - HALVES + 1)
                half = y_sum[:, s * HALF:(s + 1) * HALF]
                nc.gpsimd.tensor_tensor(half, half, y_stash[:, m, :], ALU.add).then_inc(stash_added, 1)
            pool.wait_ge(stash_added, 2 * HALVES)
            for m in range(last, last + HALVES):
                add_up(m, m % HALVES)

        @block.scalar
        def _(act):
            act.dma_start(pa[:], par_a).then_inc(ld_pa, 16)
            act.dma_start(pb[:], par_b).then_inc(ld_pb, 16)

            def copy_ctx(b):
                c = A("ctx")[:, b * KEYS:(b + 1) * KEYS]
                o = ctx_rep[:, b, :].rearrange("p (g w) -> p g w", w=GWIDTH)[:, :, 0:GCOLS]
                nc.scalar.activation(o.rearrange("p g (h k) -> p g h k", k=KEYS),
                                     c.unsqueeze(1).unsqueeze(1).broadcast_to([P, GROUPS, GH, KEYS]), ACT.Copy)\
                    .then_inc(ctx_copied, 1)

            def copy_norm(n):
                a, b = Q_PIECES[n]
                act.wait_ge(norm_turned, n + 1)
                nc.scalar.activation(xnT[:, a:b], norm_piece(n), ACT.Copy)\
                    .then_inc(norm_copied, 1)

            def high_q(n):
                a, b = Q_PIECES[n]
                act.wait_ge(q_projected, n + 1)
                nc.scalar.activation(q_hi[:, a:b], q_piece(n), ACT.Identity, bias=A("bq")).then_inc(q_hi_done, 1)

            def high_keys(b):
                for j in range(GH):
                    nc.scalar.activation(kb_hi[:, b, j * KEYS:(j + 1) * KEYS], kt_hi[:, b, :].bitcast(f32),
                                         ACT.Copy, scale=C("head")[:, j:j + 1]).then_inc(kb_hi_done, 1)

            def biases(i):
                nc.scalar.activation(b1_pair[:], pb[:, bass.ds(i * (2 * HCH) + col_b["b1"][0], 2 * HCH)],
                                     ACT.Copy).then_inc(b1_here, 1)
                act.wait_ge(b1_here, i + 1)

            act.wait_ge(consts_set, 1)
            nc.scalar.activation(table[:], neg_half[:, 0:1], ACT.Exp).then_inc(table_loaded, 1)
            act.wait_ge(ld_pa, 16)
            act.wait_ge(ld_cst, 16)
            act.wait_ge(kt_hi_done, 1)
            high_keys(0)
            copy_norm(0)
            high_q(0)
            copy_norm(1)
            copy_ctx(0)
            high_q(1)
            high_keys(1)

            def exps(t):
                for j in range(QUADS):
                    u = QUADS * t + j
                    act.wait_ge(turned, u + 1)
                    if t >= 2 and j == 0:
                        act.wait_ge(weighted, t - 1)
                    nc.scalar.activation(probs[:, t % 2, j * QUAD * P:(j + 1) * QUAD * P],
                                         turned_bank[u % 2][:], ACT.Exp,
                                         scale=SCALE).then_inc(exp_done, 1)

            def high_x2(t):
                act.wait_ge(xn2_turned, t + 1)
                nc.scalar.activation(x2_hi[:, t * P:(t + 1) * P], turned_x2, ACT.Copy)\
                    .then_inc(x2_hi_done, 1)

            def hidden(n, j, first):
                u, c, r = j // STEPS, j % HCH, j % RING
                act.wait_ge(up_done, n + 1)
                nc.scalar.activation(score[:, r, :], score[:, r, :], ACT.Gelu,
                                     bias=b1_pair[:, u * HCH + c:u * HCH + c + 1]).then_inc(gelu_done, 1)
                act.wait_ge(gelu_done, n + 1)
                if not first:
                    act.wait_ge(down_done, n - (RING - 1))
                nc.scalar.activation(h_hi[:, r, :], score[:, r, :], ACT.Copy).then_inc(h_hi_done, 1)

            for k in range(TILES + 4):
                if 0 <= k - 1 < TILES:
                    exps(k - 1)
                if k == 1:
                    copy_ctx(1)
                    copy_norm(2)
                    act.wait_ge(ld_pb, 16)
                    biases(0)
                if k == 2:
                    high_q(2)
                if 0 <= k - 4 < TILES:
                    high_x2(k - 4)
                for j in DRAIN_HIDDEN.get(k, ()):
                    hidden(j, j, True)
            for j in range(sum(map(len, DRAIN_HIDDEN.values())), PAIR):
                hidden(j, j, j < RING)
                if j == TANH_AT:
                    act.wait_ge(logits_shifted, 1)
                    nc.scalar.activation(r_e[:], r_l[:], ACT.Tanh, scale=1.0 / 8).then_inc(tanh_done, 1)
                if j == SQUARE_AT:
                    act.wait_ge(root_done, 1)
                    nc.scalar.activation(r_c[:], r_c[:], ACT.Square).then_inc(squared, 1)
                    act.wait_ge(squared, 1)
                    nc.scalar.activation(r_c[:], r_c[:], ACT.Square).then_inc(squared, 1)
                if j == GATE_COPY_AT:
                    act.wait_ge(gate_turned, 1)
                    nc.scalar.activation(gateT[:], gate_turn, ACT.Copy).then_inc(gateT_done, 1)
                    act.wait_ge(gateT_done, 1)
                    act.dma_start(gate_rows.rearrange("e (t p) -> t e p", p=P), gateT[:])\
                        .then_inc(gate_stored, 16)
                if j == GATE_STORE_AT:
                    act.wait_ge(gate_stored, 16)
                    for e in [*range(2, EXPERTS), 0, 1]:
                        act.dma_start(gate_all[:, e, :], gate_rows[e, :].partition_broadcast(P))\
                            .then_inc(gate_spread[e], 16)
            with act.Fori(1, EXPERTS // 2) as i:
                biases(i)
                for j in range(PAIR):
                    hidden(i * PAIR + j, j, False)

        @block.vector
        def _(dve):
            chain = [0]

            def link(ins):
                chain[0] += 1
                ins.then_inc(dve_chain, 1)
                dve.wait_ge(dve_chain, chain[0])

            def bc(ap, shape):
                return ap.broadcast_to(shape)

            def moments(s):
                dve.wait_ge(ld_x0 if s == 0 else ld_x1, 16)
                for t in range(s * HT, (s + 1) * HT):
                    nc.vector.bn_stats(stats[:, t, :], X[:, t, :]).then_inc(stats_done, 1)
                for t in range(s * HT, (s + 1) * HT):
                    dve.wait_ge(stats_done, t + 1)
                    nc.vector.bn_aggr(mv[:, t, :], stats[:, t, :]).then_inc(moments_done, 1)

            def normalise(s):
                dve.wait_ge(rstd_done, s + 1)
                for t in range(s * HT, (s + 1) * HT):
                    nc.vector.tensor_scalar(xn[:, t, :], X[:, t, :], mv[:, t, 0:1], rstd[:, t:t + 1],
                                            ALU.subtract, ALU.mult).then_inc(normed, 1)

            def low_q(n):
                a, b = Q_PIECES[n]
                dve.wait_ge(q_hi_done, n + 1)
                nc.vector.scalar_tensor_tensor(out=q_lo[:, a:b], in0=q_piece(n), scalar=A("bq"),
                                               in1=q_hi[:, a:b].bitcast(f32), op0=ALU.add, op1=ALU.subtract)\
                    .then_inc(q_done, 1)

            def values(b):
                dve.wait_ge(values_projected, b + 1)
                if b == 0:
                    dve.wait_ge(ld_bv, 16)
                    dve.wait_ge(v_ones_set, 1)
                nc.vector.tensor_tensor(v_sum[:], values_bank, bv_all[:], ALU.add).then_inc(v_sum_done, 1)
                dve.wait_ge(v_sum_done, b + 1)
                nc.vector.tensor_tensor(v_blk[:, b].rearrange("p n w -> p (n w)"), v_sum[:],
                                        v_ones[:].rearrange("p n w -> p (n w)"), ALU.mult)\
                    .then_inc(values_set, 1)

            nc.vector.memset(warm[:], 1.0).then_inc(warm_set, 1)
            moments(0)
            dve.wait_ge(keys_projected, 1)
            kt = mixed_bank[:, 0:BATCH * KEYS].rearrange("p (b k) -> p b k", b=BATCH)
            nc.vector.tensor_scalar(kt_hi[:], kt, A("bk"), None, ALU.add).then_inc(kt_hi_done, 1)
            dve.wait_ge(kt_hi_done, 1)
            nc.vector.scalar_tensor_tensor(out=kt_lo[:], in0=kt, scalar=A("bk"), in1=kt_hi[:].bitcast(f32),
                                           op0=ALU.add, op1=ALU.subtract).then_inc(kt_done, 1)
            normalise(0)
            low_q(0)
            moments(1)
            dve.wait_ge(zeros_set, 2)

            def pair_view(ap3):
                return ap3.rearrange("p g (h k) -> p g h k", k=KEYS)

            def maximum(t, a):
                dve.wait_ge(scored, 2 * t + a + 1)
                nc.vector.tensor_reduce(
                    mx[:, t % 2, 2 * a * GH:2 * (a + 1) * GH].rearrange("p (g h) -> p g h", g=2),
                    pair_view(score[:, 2 * a:2 * a + 2, 0:GCOLS]), AX.X, ALU.max).then_inc(max_done, 1)

            def shift(t, a):
                dve.wait_ge(max_done, 2 * t + a + 1)
                if t >= 2 and a == 0:
                    dve.wait_ge(turned, QUADS * (t - 1))
                s = pair_view(score[:, 2 * a:2 * a + 2, 0:GCOLS])
                o = pair_view(shifted[:, t % 2, 2 * a * GWIDTH:2 * (a + 1) * GWIDTH]
                              .rearrange("p (g w) -> p g w", w=GWIDTH)[:, :, 0:GCOLS])
                m = mx[:, t % 2, 2 * a * GH:2 * (a + 1) * GH].rearrange("p (g h) -> p g h", g=2)
                nc.vector.tensor_tensor(o, s, bc(m.unsqueeze(3), [P, 2, GH, KEYS]), ALU.subtract)\
                    .then_inc(shift_done, 1)

            def reciprocal(t):
                dve.wait_ge(weighted, t + 1)
                nc.vector.reciprocal(rec[:, t % 2, :], out_bank[:, P:2 * P]).then_inc(rec_done, 1)

            def divide(t):
                dve.wait_ge(rec_done, t + 1)
                if t >= 2:
                    dve.wait_ge(projected, t - 1)
                nc.vector.tensor_tensor(attnT[:, t % 2, :], out_bank[:, 0:P], rec[:, t % 2, :], ALU.mult)\
                    .then_inc(attn_done, 1)

            def residual(t):
                dve.wait_ge(projected, t + 1)
                if t % HT == 0:
                    dve.wait_ge(bo_added, t // HT + 1)
                nc.vector.tensor_tensor(X1[:, t, :], projection, Xb[:, t, :], ALU.add)\
                    .then_inc(x1_done, 1)

            def stats_of(t):
                dve.wait_ge(x1_done, t + 1)
                nc.vector.bn_stats(stats2[:, t % 2, :], X1[:, t, :]).then_inc(stats2_done, 1)

            def moments_of(t):
                dve.wait_ge(stats2_done, t + 1)
                if t >= 2:
                    dve.wait_ge(xn2_done, t - 1)
                nc.vector.bn_aggr(mv2[:, t % 2, :], stats2[:, t % 2, :]).then_inc(moments2_done, 1)

            def low_x2(t):
                dve.wait_ge(x2_hi_done, t + 1)
                nc.vector.tensor_tensor(x2_lo[:, t * P:(t + 1) * P], turned_x2,
                                        x2_hi[:, t * P:(t + 1) * P].bitcast(f32), ALU.subtract)\
                    .then_inc(x2_done, 1)

            def low(n, r):
                dve.wait_ge(h_hi_done, n + 1)
                nc.vector.tensor_tensor(h_lo[:, r, :], score[:, r, :], h_hi[:, r, :].bitcast(f32),
                                        ALU.subtract).then_inc(h_done, 1)

            for k in range(TILES + 4):
                if 0 <= k - 3 < TILES:
                    reciprocal(k - 3)
                    divide(k - 3)
                if k < TILES:
                    maximum(k, 0)
                    shift(k, 0)
                if 0 <= k - 3 < TILES:
                    residual(k - 3)
                if k < TILES:
                    maximum(k, 1)
                if 0 <= k - 4 < TILES:
                    low_x2(k - 4)
                if k == 0:
                    low_q(1)
                if k < TILES:
                    shift(k, 1)
                if 0 <= k - 3 < TILES:
                    stats_of(k - 3)
                if 0 <= k - 3 < TILES:
                    moments_of(k - 3)
                if k == 0:
                    normalise(1)
                    values(0)
                    dve.wait_ge(ld_cst, 16)
                    nc.vector.tensor_copy(upper_bf[:], C("upper")).then_inc(upper_set, 1)
                if k == 2:
                    low_q(2)
                if k == 3:
                    values(1)
                for j in DRAIN_LOW.get(k, ()):
                    low(j, j)

            def te(ap):
                return ap.rearrange("p (t e) -> p t e", e=EXPERTS)

            def cte(ap):
                return ap.rearrange("p c (t e) -> p c t e", e=EXPERTS)

            def per_tile(ap):
                return bc(ap.unsqueeze(2), [P, TILES, EXPERTS])

            rank = bc(C("rank").unsqueeze(1), [P, TILES, EXPERTS])
            top, best, top2, best2, total, den = (r_top[:, j, :] for j in range(6))
            flat = "p c n -> p (c n)"

            def shift_logits():
                dve.wait_ge(logits_done, TILES)
                link(nc.vector.tensor_reduce(top, te(logits), AX.X, ALU.max))
                nc.vector.tensor_tensor(te(r_l[:]), te(logits), per_tile(top), ALU.subtract)\
                    .then_inc(logits_shifted, 1)

            def first_choice():
                link(nc.vector.tensor_tensor(te(r_a[:]), te(logits), per_tile(top), ALU.is_equal))
                link(nc.vector.tensor_tensor(te(r_a[:]), te(r_a[:]), rank, ALU.mult))
                link(nc.vector.tensor_reduce(best, te(r_a[:]), AX.X, ALU.max))
                link(nc.vector.tensor_tensor(te(r_m[:, 0, :]), te(r_a[:]), per_tile(best), ALU.is_equal))

            def second_choice():
                link(nc.vector.scalar_tensor_tensor(out=r_b[:], in0=r_m[:, 0, :], scalar=-BIG,
                                                    in1=logits, op0=ALU.mult, op1=ALU.add))
                link(nc.vector.tensor_reduce(top2, te(r_b[:]), AX.X, ALU.max))
                link(nc.vector.tensor_tensor(te(r_a[:]), te(r_b[:]), per_tile(top2), ALU.is_equal))
                link(nc.vector.tensor_tensor(te(r_a[:]), te(r_a[:]), rank, ALU.mult))
                link(nc.vector.tensor_reduce(best2, te(r_a[:]), AX.X, ALU.max))
                nc.vector.tensor_tensor(te(r_m[:, 1, :]), te(r_a[:]), per_tile(best2), ALU.is_equal)\
                    .then_inc(masks_done, 1)

            def root_of_exp():
                dve.wait_ge(tanh_done, 1)
                link(nc.vector.tensor_scalar(r_c[:], r_e[:], -1.0, 1.0, ALU.mult, ALU.add))
                link(nc.vector.reciprocal(r_c[:], r_c[:]))
                nc.vector.scalar_tensor_tensor(out=r_c[:], in0=r_e[:], scalar=1.0, in1=r_c[:],
                                               op0=ALU.add, op1=ALU.mult).then_inc(root_done, 1)

            def gates_of_choices():
                dve.wait_ge(squared, 2)
                dve.wait_ge(masks_done, 1)
                link(nc.vector.tensor_reduce(total, te(r_c[:]), AX.X, ALU.add))
                link(nc.vector.reciprocal(total, total))
                link(nc.vector.tensor_tensor(cte(r_pm[:]), cte(r_m[:]),
                                             bc(te(r_c[:]).unsqueeze(1), [P, 2, TILES, EXPERTS]), ALU.mult))
                link(nc.vector.tensor_reduce(r_g[:], cte(r_pm[:]), AX.X, ALU.add))
                link(nc.vector.tensor_tensor(r_g[:], r_g[:], bc(total.unsqueeze(1), [P, 2, TILES]), ALU.mult))

            def weights_of_choices():
                link(nc.vector.tensor_tensor(den, r_g[:, 0, :], r_g[:, 1, :], ALU.add))
                link(nc.vector.tensor_scalar(den, den, GATE_EPS, None, ALU.add))
                link(nc.vector.reciprocal(den, den))
                link(nc.vector.tensor_tensor(r_g[:], r_g[:], bc(den.unsqueeze(1), [P, 2, TILES]), ALU.mult))

            def drop_beyond_capacity():
                dve.wait_ge(placed, 1)
                link(nc.vector.tensor_tensor(r_pm[:].rearrange(flat), place, r_m[:].rearrange(flat), ALU.mult))
                link(nc.vector.tensor_reduce(r_pos[:], cte(r_pm[:]), AX.X, ALU.add))
                link(nc.vector.tensor_scalar(r_pos[:], r_pos[:], float(CAPACITY), None, ALU.is_lt))
                link(nc.vector.tensor_tensor(r_g[:], r_g[:], r_pos[:], ALU.mult))
                link(nc.vector.tensor_tensor(cte(r_wm[:]), cte(r_m[:]),
                                             bc(r_g[:].unsqueeze(3), [P, 2, TILES, EXPERTS]), ALU.mult))
                nc.vector.tensor_tensor(gate[:], r_wm[:, 0, :], r_wm[:, 1, :], ALU.add).then_inc(gate_done, 1)

            def stash(m):
                dve.wait_ge(down_done, HCH * (m + 1))
                nc.vector.tensor_copy(y_stash[:, m, :], y_bank[m % HALVES][:]).then_inc(y_stashed, 1)

            def gated(m, e, s, first):
                dve.wait_ge(down_done, m * HCH + HCH)
                if not first:
                    dve.wait_ge(y_added, m - (2 * HALVES + 1))
                nc.vector.tensor_tensor(
                    y_gated[:, s, :], y_bank[s][:],
                    gate_all[:].rearrange("p e t -> p (e t)")[:, bass.ds(e * TOKENS + s * HALF, HALF)],
                    ALU.mult).then_inc(y_gated_done, 1)

            between = {SHIFT_AT: shift_logits, FIRST_AT: first_choice, SECOND_AT: second_choice,
                       ROOT_AT: root_of_exp, GATES_AT: gates_of_choices, WEIGHTS_AT: weights_of_choices,
                       DROP_AT: drop_beyond_capacity}
            for j in range(PAIR):
                if j >= sum(map(len, DRAIN_LOW.values())):
                    low(j, j % RING)
                if j in between:
                    between[j]()
                if j % HCH == 1 and j > HCH:
                    stash(j // HCH - 1)

            def pair(i, first):
                for j in range(PAIR):
                    low(i * PAIR + j, j % RING)
                    m = j // HCH - 1
                    if j == 1 and first:
                        stash(2 * HALVES - 1)
                        for e in range(2, EXPERTS):
                            dve.wait_ge(gate_spread[e], 16)
                    elif j % HCH == 1:
                        gated(i * 4 + m, i * 2 + (m // HALVES), m % HALVES, first and m < HALVES)

            pair(1, True)
            with dve.Fori(2, EXPERTS // 2) as i:
                pair(i, False)
            gated(2 * EXPERTS - 1, EXPERTS - 1, 1, False)
            for s in range(HALVES):
                dve.wait_ge(final_done, s + 1)
                nc.vector.tensor_tensor(
                    result[:, s * HT:(s + 1) * HT, :].rearrange("p t e -> p (t e)"), final_bank[s][:],
                    X1[:, s * HT:(s + 1) * HT, :].rearrange("p t e -> p (t e)"), ALU.add)\
                    .then_inc(result_done, 1)

        @block.tensor
        def _(pe):
            mm, turn = nc.tensor.matmul, nc.tensor.transpose
            ident = C("ident")

            def three(o, w_hi, w_lo, m_hi, m_lo, start, stop):
                mm(o, w_lo, m_hi, start=start, stop=False)
                mm(o, w_hi, m_lo, start=False, stop=False)
                return mm(o, w_hi, m_hi, start=False, stop=stop)

            def turn_norm(n):
                a, b = Q_PIECES[n]
                for t in range(a // P, b // P):
                    pe.wait_ge(normed, t + 1)
                    last = turn(norm_piece(n)[:, t * P - a:(t + 1) * P - a], xn[:, t, :], ident)
                last.then_inc(norm_turned, 1)

            def project_q(n):
                a, b = Q_PIECES[n]
                pe.wait_ge(norm_copied, n + 1)
                mm(q_piece(n), B("wq"), xnT[:, a:b], start=True, stop=True).then_inc(q_projected, 1)

            def project_v(b):
                pe.wait_ge(ctx_copied, b + 1)
                if b == 0:
                    pe.wait_ge(zeros_set, 1)
                    pe.wait_ge(kt_done, 1)
                else:
                    pe.wait_ge(q_done, 3)
                for c in range(CHUNKS):
                    g = c // GCHUNKS
                    last = mm(values_bank[:, c * 32:(c + 1) * 32], ctx_rep[:, b, c * P:(c + 1) * P],
                              A("wv")[:, g * 32:(g + 1) * 32], start=True, stop=True)
                last.then_inc(values_projected, 1)

            pe.wait_ge(warm_set, 1)
            def keep_warm(n):
                for _ in range(n):
                    mm(score[:, 0, :], warm[:, 0:P], warm[:], start=True, stop=True)

            keep_warm(WARM_UP)
            pe.wait_ge(ld_pa, 16)
            mm(mixed_bank[:, 0:BATCH * KEYS], A("wk"), A("ctx"), start=True, stop=True)\
                .then_inc(keys_projected, 1)
            keep_warm(4)
            pe.wait_ge(ld_cst, 16)
            turn_norm(0)
            keep_warm(2)
            pe.wait_ge(ld_pb, 16)
            project_q(0)
            turn_norm(1)
            keep_warm(2)

            def scores(t):
                b, tt = t // BATCH_TILES, slice(t * P, (t + 1) * P)
                for a in range(2):
                    if t >= 1:
                        pe.wait_ge(shift_done, 2 * (t - 1) + a + 1)
                    for n, (w, m) in enumerate(((q_lo, kb_hi), (q_hi, kb_lo), (q_hi, kb_hi))):
                        for g in (2 * a, 2 * a + 1):
                            rows = slice(32 * g, 32 * (g + 1))
                            last = mm(score[:, g, 0:GCOLS], w[rows, tt], m[rows, b, :],
                                      start=(n == 0), stop=(n == 2))
                    last.then_inc(scored, 1)

            def turns(t, quads):
                for j in quads:
                    c0, c1 = j * QUAD, (j + 1) * QUAD
                    u = QUADS * t + j
                    pe.wait_ge(shift_done, 2 * t + (1 if c1 * P <= 2 * GWIDTH else 2))
                    if u >= 2:
                        pe.wait_ge(exp_done, u - 1)
                    for c in range(c0, c1):
                        last = turn(turned_bank[u % 2][:, (c - c0) * P:(c - c0 + 1) * P],
                                    shifted[:, t % 2, c * P:(c + 1) * P], ident)
                    last.then_inc(turned, 1)

            def weigh(t):
                b = t // BATCH_TILES
                if t >= 1:
                    pe.wait_ge(x1_done, t)
                pe.wait_ge(exp_done, QUADS * (t + 1))
                for what, col in ((v_ones, P), (v_blk[:, b], 0)):
                    for r in range(GCHUNKS):
                        for g in range(GROUPS):
                            c = g * GCHUNKS + r
                            last = mm(out_bank[32 * g:32 * (g + 1), col:col + P], what[:, c, :],
                                      probs[:, t % 2, c * P:(c + 1) * P],
                                      start=(r == 0), stop=(r == GCHUNKS - 1))
                last.then_inc(weighted, 1)

            def project(t):
                pe.wait_ge(attn_done, t + 1)
                mm(projection, attnT[:, t % 2, :], B("wo"), start=True, stop=True).then_inc(projected, 1)

            def turn_x2(t):
                pe.wait_ge(xn2_done, t + 1)
                if t >= 1:
                    pe.wait_ge(x2_done, t)
                turn(turned_x2, xn2[:, t % 2, :], ident).then_inc(xn2_turned, 1)

            def project_logits(t):
                pe.wait_ge(x2_done, t + 1)
                tt = slice(t * P, (t + 1) * P)
                three(logits[:, t * EXPERTS:(t + 1) * EXPERTS], x2_hi[:, tt], x2_lo[:, tt],
                      wg_hi[:], wg_lo[:], True, True).then_inc(logits_done, 1)

            def up(n, u, s, c, r, first):
                if not first:
                    pe.wait_ge(h_done, n - (RING - 1))
                cc, ss = slice(c * P, (c + 1) * P), slice(s * HALF, (s + 1) * HALF)
                three(score[:, r, :], w1_hi[:, u, cc], w1_lo[:, u, cc], x2_hi[:, ss], x2_lo[:, ss],
                      True, True).then_inc(up_done, 1)

            def down(n, m, u, s, c, r, first):
                pe.wait_ge(h_done, n + 1)
                cc = slice(c * P, (c + 1) * P)
                three(y_bank[s][:], w2_hi[:, u, cc], w2_lo[:, u, cc], h_hi[:, r, :], h_lo[:, r, :],
                      c == 0, c == HCH - 1).then_inc(down_done, 1)

            def step_up(i, j, first):
                if j % STEPS == 0:
                    pe.wait_ge(w1_split, i * 2 + (j // STEPS + 1))
                up(i * PAIR + j, j // STEPS % 2, j // HCH % HALVES, j % HCH, j % RING, first)

            def step_down(i, j, stashed, first):
                m = j // HCH
                if j % STEPS == 0:
                    pe.wait_ge(w2_split, i * 2 + (j // STEPS + 1))
                if j % HCH == 0:
                    if stashed > 0:
                        pe.wait_ge(y_stashed, stashed)
                    elif not first:
                        pe.wait_ge(y_gated_done, i * 4 + (m - 1 - 2 * HALVES))
                down(i * PAIR + j, i * 4 + m, j // STEPS, m % HALVES, j % HCH, j % RING, first)

            for k in range(TILES + 4):
                if k < TILES:
                    b = k // BATCH_TILES
                    if k % BATCH_TILES == 0:
                        pe.wait_ge(kb_hi_done, GH * (b + 1))
                        pe.wait_ge(kb_lo_done, GH * (b + 1))
                    pe.wait_ge(q_done, 1 if k == 0 else 2 + b)
                    scores(k)
                if k == 0:
                    project_q(1)
                    project_v(0)
                if 0 <= k - 1 < TILES:
                    if k == 1:
                        pe.wait_ge(norm_copied, 2)
                        pe.wait_ge(q_done, 2)
                    turns(k - 1, (0, 1))
                if 0 <= k - 4 < TILES:
                    if k == 4:
                        pe.wait_ge(values_set, 2)
                    turn_x2(k - 4)
                if 0 <= k - 3 < TILES:
                    project(k - 3)
                if 0 <= k - 1 < TILES:
                    turns(k - 1, (2,))
                if 0 <= k - 2 < TILES:
                    if k == 2:
                        pe.wait_ge(values_set, 1)
                        pe.wait_ge(v_ones_set, 1)
                    weigh(k - 2)
                if 0 <= k - 4 < TILES:
                    if k == 4:
                        pe.wait_ge(wg_done, 1)
                    project_logits(k - 4)
                if k == 1:
                    pe.wait_ge(v_sum_done, 1)
                    turn_norm(2)
                if k == 2:
                    project_q(2)
                if k == 3:
                    project_v(1)
                if k == TILES:
                    pe.wait_ge(shift_done, 2 * TILES)
                for j in DRAIN_UP.get(k, ()):
                    step_up(0, j, True)
                for j in DRAIN_DOWN.get(k, ()):
                    if j == 0:
                        pe.wait_ge(exp_done, QUADS * TILES)
                    step_down(0, j, 0, True)

            def place_choices():
                pe.wait_ge(masks_done, 1)
                pe.wait_ge(upper_set, 1)
                pe.wait_ge(consts_set, 2)
                place4 = place.rearrange("p (c t e) -> p c t e", c=2, e=EXPERTS)
                masks = r_m[:].rearrange("p c (t e) -> p c t e", e=EXPERTS)
                mm(place, upper_bf[:], r_m[:].rearrange("p c n -> p (c n)"), start=True, stop=False)
                for d in range(1, TILES):
                    mm(place4[:, :, d:TILES, :], ones_bf[:], masks[:, :, 0:TILES - d, :],
                       start=False, stop=False)
                for t in range(TILES):
                    last = mm(place4[:, 1], ones_bf[:],
                              masks[:, 0, t:t + 1, :].broadcast_to([P, TILES, EXPERTS]),
                              start=False, stop=(t == TILES - 1))
                last.then_inc(placed, 1)

            def turn_gates():
                pe.wait_ge(gate_done, 1)
                turn(gate_turn, gate[:], ident).then_inc(gate_turned, 1)

            ups = sum(map(len, DRAIN_UP.values()))
            for j in range(sum(map(len, DRAIN_DOWN.values())), PAIR):
                for n in range(ups, j + AHEAD + 1):
                    step_up(0, n, n < RING)
                ups = max(ups, j + AHEAD + 1)
                step_down(0, j, max(j // HCH - 1, 0), True)
                if j == PLACE_AT:
                    place_choices()
                if j == TURN_AT:
                    turn_gates()
            for j in range(PAIR):
                step_up(1, j + AHEAD, False)
                m = j // HCH
                step_down(1, j, 2 * HALVES - 1 + m if m < HALVES else 0, m < HALVES)
            with pe.Fori(2, EXPERTS // 2 - 1) as i:
                for j in range(PAIR):
                    step_up(i, j + AHEAD, False)
                    step_down(i, j, 0, False)

            def final_b2(s):
                mm(final_bank[s][:], gateT[:], b2_diag[:, s * HT:(s + 1) * HT, :].rearrange("p t e -> p (t e)"),
                   start=True, stop=False)

            def final_add(s, src, stop):
                for t in range(HT):
                    last = mm(final_bank[s][:, t * P:(t + 1) * P], src[:, t * P:(t + 1) * P], ident,
                              start=False, stop=stop and t == HT - 1)
                return last

            for j in range(PAIR):
                if j + AHEAD < PAIR:
                    step_up(EXPERTS // 2 - 1, j + AHEAD, False)
                step_down(EXPERTS // 2 - 1, j, 0, False)
                if j == 2:
                    pe.wait_ge(ld_b2, 16)
                    pe.wait_ge(gateT_done, 1)
                    for s in range(HALVES):
                        final_b2(s)
            for s in range(HALVES):
                pe.wait_ge(stash_added, HALVES + s + 1)
                pe.wait_ge(y_added, 2 * EXPERTS - 3 * HALVES + s - 1)
                final_add(s, y_sum[:, s * HALF:(s + 1) * HALF], False)
                pe.wait_ge(y_gated_done, 2 * EXPERTS - 3 * HALVES + s + 1)
                final_add(s, y_gated[:, s, :], True).then_inc(final_done, 1)


def constants():
    import numpy as np
    ident = np.eye(P)
    head = np.arange(P)[:, None] // HEAD_DIM % GH == np.arange(GH)[None, :]
    row = np.arange(CHUNKS)[None, :] % GCHUNKS * P + np.arange(P)[:, None]
    vmask = (row[:, :, None] // KEYS == np.arange(GH)).reshape(P, CHUNKS * GH)
    upper = np.arange(P)[:, None] < np.arange(P)[None, :]
    rank = np.broadcast_to(EXPERTS - np.arange(EXPERTS), (P, EXPERTS))
    return np.concatenate([ident, head, vmask, upper, rank], axis=1).astype(np.float32)


def kernel(x, ctx_1024, mask_BxSxS2_if1, L0_xattn_Wq, L0_xattn_bq, L0_xattn_Wk, L0_xattn_bk,
           L0_xattn_Wv, L0_xattn_bv, L0_xattn_Wo, L0_xattn_bo, L0_ffn_Wg, L0_ffn_W1, L0_ffn_b1,
           L0_ffn_W2, L0_ffn_b2):
    import numpy as np
    import concourse.bacc as bacc
    from concourse.bass_utils import run_bass_kernel_spmd

    a = np.asarray
    ctx_t = a(ctx_1024).reshape(BATCH * KEYS, EMB).T
    par_a = np.concatenate([a(L0_xattn_Wk).T, ctx_t, a(L0_xattn_Wv).T, a(L0_xattn_bk)[:, None],
                            a(L0_xattn_bq)[:, None]], axis=1)
    par_b = np.concatenate([a(L0_xattn_Wq).T, a(L0_xattn_Wo).T, a(L0_ffn_Wg),
                            a(L0_ffn_b1).reshape(EXPERTS * HCH, P).T], axis=1)
    bias_v = np.concatenate([a(L0_xattn_bv)[32 * g:32 * (g + 1)] for g in np.arange(CHUNKS) // GCHUNKS])
    b2_diag = np.zeros((TILES, EXPERTS, TILES, EMB), np.float32)
    for t in range(TILES):
        b2_diag[t, :, t, :] = a(L0_ffn_b2)
    arrays = {
        "x": a(x).reshape(TOKENS, EMB), "par_a": par_a, "par_b": par_b, "bias_v": bias_v,
        "bias_o": a(L0_xattn_bo), "w1": a(L0_ffn_W1), "w2": a(L0_ffn_W2), "b2": b2_diag.reshape(TE, TILES, EMB),
        "const": constants(),
    }
    arrays = {f"in_{k}": np.ascontiguousarray(v) for k, v in arrays.items()}
    nc = bacc.Bacc("TRN2", target_bir_lowering=False, num_devices=1)
    args = [nc.dram_tensor(k, v.shape, mybir.dt.from_np(v.dtype), kind="ExternalInput").ap()
            for k, v in arrays.items()]
    args.append(nc.dram_tensor("out_0", (TOKENS, EMB), mybir.dt.float32, kind="ExternalOutput").ap())
    xattn_moe(nc, *args)
    r = run_bass_kernel_spmd(nc, [arrays], core_ids=[0])
    return r.results[0]["out_0"].reshape(BATCH, SEQ, EMB)
```

```python
import concourse.bass as bass
from concourse import mybir
from contextlib import ExitStack


BATCH, SEQ, EMB = 2, 512, 128
KEYS = 77
HEADS = 16
HEAD_DIM = EMB // HEADS
EXPERTS = 8
HIDDEN = 512
TOP_K = 2
TOKENS = BATCH * SEQ
CAPACITY = 2 * TOP_K * TOKENS // EXPERTS
P = 128
TILES = TOKENS // P
BATCH_TILES = SEQ // P
HALF = 512
HALVES = TOKENS // HALF
HT = HALF // P
PIECE = HALF // 2

GH = 32 // HEAD_DIM
GROUPS = HEADS // GH
GCOLS = GH * KEYS
GCHUNKS = -(-GCOLS // P)
GWIDTH = GCHUNKS * P
CHUNKS = GROUPS * GCHUNKS
WIDTH = CHUNKS * P
QUAD = 4
QUADS = CHUNKS // QUAD

HCH = HIDDEN // P
STEPS = HALVES * HCH
RING = 4
AHEAD = 3
PAIR = 2 * STEPS
LN_EPS = 1e-5
GATE_EPS = 1e-9
BIG = 3.0e38
TE = TILES * EXPERTS

PAR_A = [("wk", EMB), ("ctx", BATCH * KEYS), ("wv", EMB), ("bk", 1), ("bq", 1), ("bv", 1)]
PAR_B = [("wq", EMB), ("wo", EMB), ("wg", EXPERTS), ("b1", EXPERTS * HCH), ("b2", EXPERTS)]
CONST = [("ident", P), ("head", GH), ("vmask", GCHUNKS * GH), ("upper", P), ("rank", EXPERTS)]


def columns(parts):
    at, out = 0, {}
    for name, width in parts:
        out[name] = (at, at + width)
        at += width
    return out, at


def xattn_moe(nc, x, par_a, par_b, bias_o, w1, w2, const, out):
    f32, f32r, bf16 = mybir.dt.float32, mybir.dt.float32r, mybir.dt.bfloat16
    ALU, ACT, AX = mybir.AluOpType, mybir.ActivationFunctionType, mybir.AxisListType
    SCALE = float(HEAD_DIM) ** -0.5
    col_a, width_a = columns(PAR_A)
    col_b, width_b = columns(PAR_B)
    col_c, width_c = columns(CONST)

    ctx = ExitStack()
    with ctx:
        def sb(name, shape, dt=f32):
            return ctx.enter_context(nc.sbuf_tensor(name, shape, dt))

        def sems(names):
            return [ctx.enter_context(nc.semaphore(n)) for n in names.split()]

        pa = sb("pa", [P, width_a])
        pb = sb("pb", [P, width_b])
        cst = sb("cst", [P, width_c])

        def A(name):
            return pa[:, col_a[name][0]:col_a[name][1]]

        def B(name):
            return pb[:, col_b[name][0]:col_b[name][1]]

        def C(name):
            return cst[:, col_c[name][0]:col_c[name][1]]

        X = sb("X", [P, TILES, EMB])
        bv_rep = sb("bv_rep", [P, P])
        bo_all = sb("bo_all", [P, EMB])
        bias_all = sb("bias_all", [P, EMB])
        neg_mean = sb("neg_mean", [P, HT])
        neg_half = sb("neg_half", [P, TILES])
        Xb = sb("Xb", [P, TILES, EMB])
        X1 = sb("X1", [P, TILES, EMB])
        stats = sb("stats", [P, TILES, 6])
        mv = sb("mv", [P, TILES, 2])
        rstd = sb("rstd", [P, TILES])
        xn = sb("xn", [P, TILES, EMB])
        xnT = sb("xnT", [P, TOKENS])
        q_hi = sb("q_hi", [P, TOKENS], f32r)
        q_lo = sb("q_lo", [P, TOKENS], f32r)
        kt_hi = sb("kt_hi", [P, BATCH, KEYS], f32r)
        kt_lo = sb("kt_lo", [P, BATCH, KEYS], f32r)
        kb_hi = sb("kb_hi", [P, BATCH, GCOLS], f32r)
        kb_lo = sb("kb_lo", [P, BATCH, GCOLS], f32r)
        ctx_rep = sb("ctx_rep", [P, BATCH, GWIDTH])
        v_blk = sb("v_blk", [P, BATCH, GCHUNKS, EMB])
        v_ones = sb("v_ones", [P, GCHUNKS, 32])
        mx = sb("mx", [P, 2, HEADS])
        shifted = sb("shifted", [P, 2, WIDTH])
        probs = sb("probs", [P, 2, WIDTH])
        rec = sb("rec", [P, 2, P])
        attnT = sb("attnT", [P, 2, P])
        stats2 = sb("stats2", [P, 2, 6])
        mv2 = sb("mv2", [P, 2, 2])
        ln2 = sb("ln2", [P, 2, 3])
        xn2 = sb("xn2", [P, 2, EMB])
        x2_hi = sb("x2_hi", [P, TOKENS], f32r)
        x2_lo = sb("x2_lo", [P, TOKENS], f32r)
        wg_hi = sb("wg_hi", [P, EXPERTS], f32r)
        wg_lo = sb("wg_lo", [P, EXPERTS], f32r)
        warm = sb("warm", [P, 512], bf16)
        table = sb("table", [P, 1])
        ones_bf = sb("ones_bf", [P, P], bf16)
        upper_bf = sb("upper_bf", [P, P], bf16)
        r_l = sb("r_l", [P, TE])
        r_e = sb("r_e", [P, TE])
        r_a = sb("r_a", [P, TE])
        r_b = sb("r_b", [P, TE])
        r_c = sb("r_c", [P, TE])
        r_m = sb("r_m", [P, 2, TE], bf16)
        r_top = sb("r_top", [P, 6, TILES])
        r_g = sb("r_g", [P, 2, TILES])
        r_pm = sb("r_pm", [P, 2, TE])
        r_pos = sb("r_pos", [P, 2, TILES])
        r_wm = sb("r_wm", [P, 2, TE])
        gate = sb("gate", [P, TE])
        gateT = sb("gateT", [TE, P])
        gate_all = sb("gate_all", [P, EXPERTS, TOKENS])
        w1_raw = sb("w1_raw", [P, 2, HIDDEN])
        w2_raw = sb("w2_raw", [P, 2, HCH * EMB])
        w1_hi = sb("w1_hi", [P, 2, HIDDEN], f32r)
        w1_lo = sb("w1_lo", [P, 2, HIDDEN], f32r)
        w2_hi = sb("w2_hi", [P, 2, HCH * EMB], f32r)
        w2_lo = sb("w2_lo", [P, 2, HCH * EMB], f32r)
        b1_pair = sb("b1_pair", [P, 2 * HCH])
        h_hi = sb("h_hi", [P, RING, HALF], f32r)
        h_lo = sb("h_lo", [P, RING, HALF], f32r)
        y_stash = sb("y_stash", [P, 2 * HALVES, HALF])
        y_gated = sb("y_gated", [P, HALVES, HALF])
        y_sum = sb("y_sum", [P, TOKENS])
        result = sb("result", [P, TILES, EMB])

        score = ctx.enter_context(nc.psum_tensor("score", [P, GROUPS, 512], f32))
        bank = {i: ctx.enter_context(nc.psum_tensor(f"bank{i}", [P, 512], f32)) for i in range(4, 8)}
        turned_bank = [bank[4], bank[5]]
        out_bank, mixed_bank = bank[6], bank[7]
        y_bank = [bank[4], bank[5]]
        final_bank = [bank[6], bank[7]]
        last_bank = [bank[4], score[:, 0, :]]
        turned_x2 = mixed_bank[:, 0:P]
        logits = mixed_bank[:, P:P + TE]
        projection = out_bank[:, 2 * P:3 * P]
        place = out_bank[:, 0:2 * TE]
        gate_turn = out_bank[0:TE, 2 * P:3 * P]

        ld_pa, ld_pb, ld_cst, ld_x0, ld_x1, ld_bo = sems(
            "ld_pa ld_pb ld_cst ld_x0 ld_x1 ld_bo")
        pool_chain, dve_chain, consts_set, zeros_set, v_ones_set, warm_set = sems(
            "pool_chain dve_chain consts_set zeros_set v_ones_set warm_set")
        keys_projected, kt_hi_done, kt_done, kb_hi_done, kb_lo_done = sems(
            "keys_projected kt_hi_done kt_done kb_hi_done kb_lo_done")
        ctx_copied, values_projected, values_set, bv_spread, bias_projected, bias_summed = sems(
            "ctx_copied values_projected values_set bv_spread bias_projected bias_summed")
        stats_done, moments_done, rstd_done, normed, normed_late, norm_turned, norm_copied = sems(
            "stats_done moments_done rstd_done normed normed_late norm_turned norm_copied")
        q_projected, q_hi_done, q_done, bo_added, upper_set, wg_done = sems(
            "q_projected q_hi_done q_done bo_added upper_set wg_done")
        scored, max_done, shift_done, turned, exp_done = sems(
            "scored max_done shift_done turned exp_done")
        weighted, rec_done, attn_done, projected, x1_done = sems(
            "weighted rec_done attn_done projected x1_done")
        stats2_done, moments2_done, xn2_done, xn2_turned, x2_hi_done, x2_done = sems(
            "stats2_done moments2_done xn2_done xn2_turned x2_hi_done x2_done")
        logits_done, logits_shifted, tanh_done, root_done, squared = sems(
            "logits_done logits_shifted tanh_done root_done squared")
        masks_done, placed, weights_done, gate_done = sems("masks_done placed weights_done gate_done")
        gate_turned, gateT_done, gate_stored = sems("gate_turned gateT_done gate_stored")
        gate_spread = sems(" ".join(f"gate_spread{i}" for i in range(EXPERTS)))
        w1_loaded = sems("w1_loaded0 w1_loaded1")
        w2_loaded = sems("w2_loaded0 w2_loaded1")
        waits_over, w_hi_done, w1_split, w2_split = sems("waits_over w_hi_done w1_split w2_split")
        b1_here, up_done, gelu_done, h_hi_done, h_hi_dve_done, h_done, down_done = sems(
            "b1_here up_done gelu_done h_hi_done h_hi_dve_done h_done down_done")
        y_stashed, stash_gated, stash_added, y_gated_done, y_added, piece_gated = sems(
            "y_stashed stash_gated stash_added y_gated_done y_added piece_gated")
        final_done, result_begun, result_done, stored = sems("final_done result_begun result_done stored")

        gate_rows = nc.dram_tensor("gate_rows", (EXPERTS, TOKENS), f32, kind="Internal").ap()
        x_v = x.rearrange("(t p) e -> p t e", p=P)
        out_v = out.rearrange("(t p) e -> p t e", p=P)
        w1_v = w1.rearrange("e d f -> d e f")
        w2_v = w2.rearrange("e (c p) d -> p e c d", p=P)

        SHIFT_AT, ROOT_AT, FIRST_AT, SECOND_AT, GATES_AT, WEIGHTS_AT, PLACES_AT = 4, 6, 7, 8, 11, 12, 14
        TANH_AT, SQUARE_AT = 6, 9
        PLACE_AT, TURN_AT = 11, 15
        WARM_UP = 7
        DVE_HIGH = HCH - 1
        DVE_HIGHS = PAIR // HCH
        LOGITS_LAG = 5
        FIRST, MIDDLE, LAST = range(3)
        DRAIN_HIDDEN = {(TILES + 1, FIRST): [0], (TILES + 1, LAST): [1], (TILES + 2, FIRST): [2, 3],
                        (TILES + 2, LAST): [4], (TILES + 3, LAST): [5]}
        DRAIN_LOW = {(TILES + 1, LAST): [0], (TILES + 2, FIRST): [1], (TILES + 2, MIDDLE): [2],
                     (TILES + 2, LAST): [3], (TILES + 3, FIRST): [4]}
        DRAIN_UP = {(TILES, FIRST): [0], (TILES, LAST): [1], (TILES + 1, MIDDLE): [2], (TILES + 1, LAST): [3],
                    (TILES + 2, MIDDLE): [4], (TILES + 2, LAST): [5], (TILES + 3, FIRST): [6]}
        DRAIN_DOWN = {(TILES + 1, LAST): [0], (TILES + 2, MIDDLE): [1], (TILES + 2, LAST): [2],
                      (TILES + 3, MIDDLE): [3]}

        def drained(steps):
            return sum(map(len, steps.values()))

        Q_PIECES = [(0, P), (P, HALF), (HALF, TOKENS)]

        def norm_piece(n):
            a, b = Q_PIECES[n]
            return (bank[4], bank[5], mixed_bank)[n][:, 0:b - a]

        def q_piece(n):
            a, b = Q_PIECES[n]
            return (out_bank, bank[4], mixed_bank)[n][:, 0:b - a]

        values_bank = [b_[:, 0:GCHUNKS * EMB] for b_ in (mixed_bank, out_bank)]

        def expert_0(j):
            return j // HCH % 2

        def half_0(j):
            return j // STEPS

        bias_bank = out_bank[:, GCHUNKS * EMB:(GCHUNKS + 1) * EMB]

        block = ctx.enter_context(nc.Block())

        @block.sync
        def _(sp):
            sp.dma_start(X[:, 0:HT, :], x_v[:, 0:HT, :]).then_inc(ld_x0, 16)
            sp.dma_start(cst[:], const).then_inc(ld_cst, 16)
            sp.dma_start(X[:, HT:TILES, :], x_v[:, HT:TILES, :]).then_inc(ld_x1, 16)

            def load_expert(e, u):
                sp.dma_start(w1_raw[:, u, :], w1_v[:, bass.ds(e, 1), :].rearrange("p a f -> p (a f)"))\
                    .then_inc(w1_loaded[u], 16)
                sp.dma_start(w2_raw[:, u, :].rearrange("p (c d) -> p c d", c=HCH),
                             w2_v[:, bass.ds(e, 1), :, :].rearrange("p a c d -> p (a c) d"))\
                    .then_inc(w2_loaded[u], 16)

            sp.dma_start(bo_all[:], bias_o.partition_broadcast(P)).then_inc(ld_bo, 16)
            for e in range(2):
                load_expert(e, e)
            for e in range(2, 4):
                sp.wait_ge(w1_split, e - 1)
                sp.wait_ge(w2_split, e - 1)
                load_expert(e, e % 2)
            sp.wait_ge(gateT_done, 1)
            sp.dma_start(gate_rows.rearrange("e (t p) -> t e p", p=P), gateT[:]).then_inc(gate_stored, 16)
            sp.wait_ge(gate_stored, 16)

            def spread(e):
                sp.dma_start(gate_all[:, e, :], gate_rows[e, :].partition_broadcast(P))\
                    .then_inc(gate_spread[e], 16)

            spread(2)
            spread(3)
            for i in range(2, EXPERTS // 2):
                for u in range(2):
                    sp.wait_ge(w1_split, i * 2 + (u - 1))
                    sp.wait_ge(w2_split, i * 2 + (u - 1))
                    load_expert(i * 2 + u, u)
                    if i == 2:
                        for e in ((4, 5, 0), (6, 7, 1))[u]:
                            spread(e)
            for n, (a, b) in enumerate(((0, HT), (HT, HT + HT // 2), (HT + HT // 2, TILES))):
                sp.wait_ge(result_done, n + 1)
                sp.dma_start(out_v[:, a:b, :], result[:, a:b, :]).then_inc(stored, 16)
            sp.wait_ge(stored, 16 * (HALVES + 1))

        @block.gpsimd
        def _(pool):
            chain = [0]

            def link(ins):
                chain[0] += 1
                ins.then_inc(pool_chain, 1)
                pool.wait_ge(pool_chain, chain[0])

            nc.gpsimd.memset(neg_half[:], -0.5).then_inc(consts_set, 1)
            nc.gpsimd.memset(ctx_rep[:, :, GCOLS:], 0.0).then_inc(zeros_set, 1)
            nc.gpsimd.memset(shifted[:].rearrange("p b (g w) -> p (b g) w", w=GWIDTH)[:, :, GCOLS:], 0.0)\
                .then_inc(zeros_set, 1)
            nc.gpsimd.memset(ones_bf[:], 1.0).then_inc(consts_set, 1)

            pool.wait_ge(consts_set, 1)

            def root(s):
                pool.wait_ge(moments_done, HT * (s + 1))
                sl = slice(s * HT, (s + 1) * HT)
                link(nc.gpsimd.tensor_scalar(rstd[:, sl], mv[:, sl, 1], LN_EPS, None, ALU.add))
                nc.gpsimd.tensor_tensor(rstd[:, sl], rstd[:, sl], neg_half[:, sl], ALU.pow)\
                    .then_inc(rstd_done, 1)

            def low_keys(b):
                for j in range(GH):
                    nc.gpsimd.tensor_scalar(kb_lo[:, b, j * KEYS:(j + 1) * KEYS], kt_lo[:, b, :].bitcast(f32),
                                            C("head")[:, j:j + 1], 1.0, ALU.mult, ALU.mult)\
                        .then_inc(kb_lo_done, 1)

            root(0)
            pool.wait_ge(ld_cst, 16)
            pool.wait_ge(kt_done, 1)
            low_keys(0)
            root(1)
            link(nc.gpsimd.tensor_scalar(neg_mean[:], mv[:, HT:TILES, 0], -1.0, None, ALU.mult))
            pool.wait_ge(rstd_done, 2)
            pool.wait_ge(ld_x1, 16)
            for t in range(HT, TILES):
                nc.gpsimd.tensor_scalar(xn[:, t, :], X[:, t, :], neg_mean[:, t - HT:t - HT + 1],
                                        rstd[:, t:t + 1], ALU.add, ALU.mult).then_inc(normed_late, 1)
            vm = C("vmask").rearrange("p (n j) -> p n j", n=GCHUNKS)
            nc.gpsimd.tensor_copy(v_ones[:].rearrange("p n (j d) -> p n j d", j=GH),
                                  vm.unsqueeze(3).broadcast_to([P, GCHUNKS, GH, HEAD_DIM])).then_inc(v_ones_set, 1)
            low_keys(1)
            pool.wait_ge(bias_summed, 1)
            pool.wait_ge(ld_x0, 16)
            for s in range(HALVES):
                sl = slice(s * HT, (s + 1) * HT)
                nc.gpsimd.tensor_tensor(Xb[:, sl, :], X[:, sl, :],
                                        bias_all[:].unsqueeze(1).broadcast_to([P, HT, EMB]), ALU.add)\
                    .then_inc(bo_added, 1)
            pool.wait_ge(ld_pb, 16)
            link(nc.gpsimd.tensor_copy(wg_hi[:], B("wg")))
            nc.gpsimd.tensor_tensor(wg_lo[:], B("wg"), wg_hi[:].bitcast(f32), ALU.subtract)\
                .then_inc(wg_done, 1)
            nc.gpsimd.tensor_copy(upper_bf[:], C("upper")).then_inc(upper_set, 1)


            def split(n, u, raw, hi, lo, loaded, level, signal):
                pool.wait_ge(loaded[u], level)
                pool.sem_inc(waits_over, 1)
                nc.gpsimd.tensor_scalar(hi[:, u, :], raw[:, u, :], 1.0, 1.0, ALU.mult, ALU.mult)\
                    .then_inc(w_hi_done, 1)
                pool.wait_ge(w_hi_done, n)
                nc.gpsimd.tensor_tensor(lo[:, u, :], raw[:, u, :], hi[:, u, :].bitcast(f32),
                                        ALU.subtract).then_inc(signal, 1)

            def norm2(t):
                p = t % 2
                pool.wait_ge(moments2_done, t + 1)
                nc.gpsimd.tensor_scalar(ln2[:, p, 0:1], mv2[:, p, 1:2], LN_EPS, None, ALU.add)\
                    .then_inc(pool_chain, 1)
                nc.gpsimd.tensor_scalar(ln2[:, p, 1:2], mv2[:, p, 0:1], -1.0, None, ALU.mult)\
                    .then_inc(pool_chain, 1)
                pool.wait_ge(pool_chain, chain[0] + 1)
                chain[0] += 2
                link(nc.gpsimd.tensor_tensor(ln2[:, p, 2:3], ln2[:, p, 0:1], neg_half[:, 0:1], ALU.pow))
                if t >= 2:
                    pool.wait_ge(xn2_turned, t - 1)
                nc.gpsimd.tensor_scalar(xn2[:, p, :], X1[:, t, :], ln2[:, p, 1:2], ln2[:, p, 2:3],
                                        ALU.add, ALU.mult).then_inc(xn2_done, 1)

            split(1, 0, w1_raw, w1_hi, w1_lo, w1_loaded, 16, w1_split)
            split(2, 0, w2_raw, w2_hi, w2_lo, w2_loaded, 16, w2_split)
            norm2(0)
            split(3, 1, w1_raw, w1_hi, w1_lo, w1_loaded, 16, w1_split)
            norm2(1)
            split(4, 1, w2_raw, w2_hi, w2_lo, w2_loaded, 16, w2_split)
            for t in range(2, TILES):
                norm2(t)
            nc.gpsimd.memset(y_sum[:], 0.0).then_inc(zeros_set, 1)
            pool.wait_ge(zeros_set, 3)

            def add_up(m, s):
                pool.wait_ge(y_gated_done, m + (1 - 2 * HALVES))
                half = y_sum[:, s * HALF:(s + 1) * HALF]
                nc.gpsimd.tensor_tensor(half, half, y_gated[:, s, :], ALU.add).then_inc(y_added, 1)

            def split_next(i, u):
                pool.wait_ge(up_done, i * PAIR + STEPS * (u + 1))
                split(i * 4 + (5 + 2 * u), u, w1_raw, w1_hi, w1_lo, w1_loaded, i * 16 + 32, w1_split)
                pool.wait_ge(down_done, i * PAIR + STEPS * (u + 1))
                split(i * 4 + (6 + 2 * u), u, w2_raw, w2_hi, w2_lo, w2_loaded, i * 16 + 32, w2_split)

            for u in range(2):
                ups_of_expert = PAIR - (1 - u) * HCH
                pool.wait_ge(up_done, ups_of_expert)
                split(5 + 2 * u, u, w1_raw, w1_hi, w1_lo, w1_loaded, 32, w1_split)
                pool.wait_ge(down_done, ups_of_expert)
                split(6 + 2 * u, u, w2_raw, w2_hi, w2_lo, w2_loaded, 32, w2_split)
                if u == 0:
                    pool.wait_ge(weights_done, 1)
                    link(nc.gpsimd.tensor_tensor(
                        r_wm[:].rearrange("p c (t e) -> p c t e", e=EXPERTS),
                        r_m[:].rearrange("p c (t e) -> p c t e", e=EXPERTS),
                        r_g[:].unsqueeze(3).broadcast_to([P, 2, TILES, EXPERTS]), ALU.mult))
                    nc.gpsimd.tensor_tensor(gate[:], r_wm[:, 0, :], r_wm[:, 1, :], ALU.add)\
                        .then_inc(gate_done, 1)

            def add_stashed(i, u):
                pool.wait_ge(y_stashed, 2 * HALVES)
                pool.wait_ge(gate_spread[u], 16)
                stashed = y_stash[:].rearrange("p m t -> p (m t)")[:, bass.ds(i * (2 * HALF) + (u - 2) * HALF, HALF)]
                gates = gate_all[:].rearrange("p e t -> p (e t)")[:, bass.ds(i * HALF + (u * TOKENS - HALF), HALF)]
                nc.gpsimd.tensor_tensor(stashed, stashed, gates, ALU.mult).then_inc(stash_gated, 1)
                pool.wait_ge(stash_gated, i * 2 + (u - 1))
                pool.wait_ge(y_added, i * 4 + (2 * u - 2))
                pool.sem_inc(waits_over, 1)
                half = y_sum[:, bass.ds(i * HALF - HALF, HALF)]
                nc.gpsimd.tensor_tensor(half, half, stashed, ALU.add).then_inc(stash_added, 1)
                pool.wait_ge(stash_added, i * 2 + (u - 1))
                pool.sem_inc(waits_over, 1)

            with pool.Fori(1, EXPERTS // 2 - 1) as i:
                for u in range(2):
                    for s in range(HALVES):
                        add_up(i * 4 + (2 * u + s), s)
                    split_next(i, u)
                    add_stashed(i, u)
            for m in range(2 * EXPERTS - 2 * HALVES, 2 * EXPERTS - 1):
                add_up(m, m % HALVES)

        @block.scalar
        def _(act):
            act.dma_start(pa[:], par_a).then_inc(ld_pa, 16)
            act.dma_start(pb[:], par_b).then_inc(ld_pb, 16)

            def copy_ctx(b):
                c = A("ctx")[:, b * KEYS:(b + 1) * KEYS]
                nc.scalar.activation(ctx_rep[:, b, 0:GCOLS].rearrange("p (h k) -> p h k", k=KEYS),
                                     c.unsqueeze(1).broadcast_to([P, GH, KEYS]), ACT.Copy)\
                    .then_inc(ctx_copied, 1)

            def copy_norm(n):
                a, b = Q_PIECES[n]
                act.wait_ge(norm_turned, n + 1)
                nc.scalar.activation(xnT[:, a:b], norm_piece(n), ACT.Copy)\
                    .then_inc(norm_copied, 1)

            def high_q(n):
                a, b = Q_PIECES[n]
                act.wait_ge(q_projected, n + 1)
                nc.scalar.activation(q_hi[:, a:b], q_piece(n), ACT.Identity, bias=A("bq")).then_inc(q_hi_done, 1)

            def high_keys(b):
                for j in range(GH):
                    nc.scalar.activation(kb_hi[:, b, j * KEYS:(j + 1) * KEYS], kt_hi[:, b, :].bitcast(f32),
                                         ACT.Copy, scale=C("head")[:, j:j + 1]).then_inc(kb_hi_done, 1)

            def biases(i):
                nc.scalar.activation(b1_pair[:], pb[:, bass.ds(i * (2 * HCH) + col_b["b1"][0], 2 * HCH)],
                                     ACT.Copy).then_inc(b1_here, 1)
                act.wait_ge(b1_here, i + 1)

            act.wait_ge(consts_set, 1)
            nc.scalar.activation(table[:], neg_half[:, 0:1], ACT.Exp)
            act.wait_ge(ld_pa, 16)
            act.wait_ge(ld_cst, 16)
            act.wait_ge(kt_hi_done, 1)
            high_keys(0)
            copy_norm(0)
            high_q(0)
            copy_norm(1)
            copy_ctx(0)
            copy_ctx(1)
            nc.scalar.activation(bv_rep[:], A("bv").broadcast_to([P, P]), ACT.Copy).then_inc(bv_spread, 1)
            high_q(1)
            high_keys(1)

            def exps(t):
                for j in range(QUADS):
                    u = QUADS * t + j
                    act.wait_ge(turned, u + 1)
                    if t >= 2 and j == 0:
                        act.wait_ge(weighted, t - 1)
                    nc.scalar.activation(probs[:, t % 2, j * QUAD * P:(j + 1) * QUAD * P],
                                         turned_bank[u % 2][:], ACT.Exp,
                                         scale=SCALE).then_inc(exp_done, 1)

            def high_x2(t):
                act.wait_ge(xn2_turned, t + 1)
                nc.scalar.activation(x2_hi[:, t * P:(t + 1) * P], turned_x2, ACT.Copy)\
                    .then_inc(x2_hi_done, 1)

            def hidden(n, j, first, u, high=True):
                c, r = j % HCH, j % RING
                act.wait_ge(up_done, n + 1)
                nc.scalar.activation(score[:, r, :], score[:, r, :], ACT.Gelu,
                                     bias=b1_pair[:, u * HCH + c:u * HCH + c + 1]).then_inc(gelu_done, 1)
                if not high:
                    return
                act.wait_ge(gelu_done, n + 1)
                if not first:
                    act.wait_ge(down_done, n - (RING - 1))
                nc.scalar.activation(h_hi[:, r, :], score[:, r, :], ACT.Copy).then_inc(h_hi_done, 1)

            for k in range(TILES + 4):
                if 0 <= k - 1 < TILES:
                    exps(k - 1)
                if k == 1:
                    copy_norm(2)
                    act.wait_ge(ld_pb, 16)
                    biases(0)
                if k == 2:
                    high_q(2)
                for j in DRAIN_HIDDEN.get((k, FIRST), []):
                    hidden(j, j, j < RING, expert_0(j))
                if 0 <= k - 4 < TILES:
                    high_x2(k - 4)
                for j in DRAIN_HIDDEN.get((k, LAST), []):
                    hidden(j, j, j < RING, expert_0(j))
            for j in range(drained(DRAIN_HIDDEN), PAIR):
                hidden(j, j, j < RING, expert_0(j))
                if j == TANH_AT:
                    act.wait_ge(logits_shifted, 1)
                    nc.scalar.activation(r_e[:], r_l[:], ACT.Tanh, scale=1.0 / 8).then_inc(tanh_done, 1)
                if j == SQUARE_AT:
                    act.wait_ge(root_done, 1)
                    nc.scalar.activation(r_c[:], r_c[:], ACT.Square).then_inc(squared, 1)
                    act.wait_ge(squared, 1)
                    nc.scalar.activation(r_c[:], r_c[:], ACT.Square).then_inc(squared, 1)
            with act.Fori(1, EXPERTS // 2) as i:
                act.wait_ge(gelu_done, i * PAIR)
                biases(i)
                for j in range(PAIR):
                    hidden(i * PAIR + j, j, False, j // STEPS, j % HCH != DVE_HIGH)

        @block.vector
        def _(dve):
            chain = [0]

            def link(ins):
                chain[0] += 1
                ins.then_inc(dve_chain, 1)
                dve.wait_ge(dve_chain, chain[0])

            def bc(ap, shape):
                return ap.broadcast_to(shape)

            def moments(s):
                dve.wait_ge(ld_x0 if s == 0 else ld_x1, 16)
                for t in range(s * HT, (s + 1) * HT):
                    nc.vector.bn_stats(stats[:, t, :], X[:, t, :]).then_inc(stats_done, 1)
                for t in range(s * HT, (s + 1) * HT):
                    dve.wait_ge(stats_done, t + 1)
                    nc.vector.bn_aggr(mv[:, t, :], stats[:, t, :]).then_inc(moments_done, 1)

            def normalise():
                dve.wait_ge(rstd_done, 1)
                for t in range(HT):
                    nc.vector.tensor_scalar(xn[:, t, :], X[:, t, :], mv[:, t, 0:1], rstd[:, t:t + 1],
                                            ALU.subtract, ALU.mult).then_inc(normed, 1)

            def low_q(n):
                a, b = Q_PIECES[n]
                dve.wait_ge(q_hi_done, n + 1)
                nc.vector.scalar_tensor_tensor(out=q_lo[:, a:b], in0=q_piece(n), scalar=A("bq"),
                                               in1=q_hi[:, a:b].bitcast(f32), op0=ALU.add, op1=ALU.subtract)\
                    .then_inc(q_done, 1)

            def values(b):
                dve.wait_ge(values_projected, b + 1)
                if b == 0:
                    dve.wait_ge(v_ones_set, 1)
                nc.vector.tensor_tensor(v_blk[:, b].rearrange("p r (g w) -> p r g w", g=GROUPS),
                                        values_bank[b].rearrange("p (r g w) -> p r g w", r=GCHUNKS, g=GROUPS),
                                        bc(v_ones[:].unsqueeze(2), [P, GCHUNKS, GROUPS, 32]), ALU.mult)\
                    .then_inc(values_set, 1)

            nc.vector.memset(warm[:], 1.0).then_inc(warm_set, 1)
            moments(0)
            dve.wait_ge(keys_projected, 1)
            kt = mixed_bank[:, 0:BATCH * KEYS].rearrange("p (b k) -> p b k", b=BATCH)
            nc.vector.tensor_scalar(kt_hi[:], kt, A("bk"), None, ALU.add).then_inc(kt_hi_done, 1)
            dve.wait_ge(kt_hi_done, 1)
            nc.vector.scalar_tensor_tensor(out=kt_lo[:], in0=kt, scalar=A("bk"), in1=kt_hi[:].bitcast(f32),
                                           op0=ALU.add, op1=ALU.subtract).then_inc(kt_done, 1)
            normalise()
            low_q(0)
            moments(1)
            dve.wait_ge(zeros_set, 2)

            def pair_view(ap3):
                return ap3.rearrange("p g (h k) -> p g h k", k=KEYS)

            def maximum(t, a):
                dve.wait_ge(scored, 2 * t + a + 1)
                nc.vector.tensor_reduce(
                    mx[:, t % 2, 2 * a * GH:2 * (a + 1) * GH].rearrange("p (g h) -> p g h", g=2),
                    pair_view(score[:, 2 * a:2 * a + 2, 0:GCOLS]), AX.X, ALU.max).then_inc(max_done, 1)

            def shift(t, a):
                dve.wait_ge(max_done, 2 * t + a + 1)
                if t >= 2 and a == 0:
                    dve.wait_ge(turned, QUADS * (t - 1))
                s = pair_view(score[:, 2 * a:2 * a + 2, 0:GCOLS])
                o = pair_view(shifted[:, t % 2, 2 * a * GWIDTH:2 * (a + 1) * GWIDTH]
                              .rearrange("p (g w) -> p g w", w=GWIDTH)[:, :, 0:GCOLS])
                m = mx[:, t % 2, 2 * a * GH:2 * (a + 1) * GH].rearrange("p (g h) -> p g h", g=2)
                nc.vector.tensor_tensor(o, s, bc(m.unsqueeze(3), [P, 2, GH, KEYS]), ALU.subtract)\
                    .then_inc(shift_done, 1)

            def reciprocal(t):
                dve.wait_ge(weighted, t + 1)
                nc.vector.reciprocal(rec[:, t % 2, :], out_bank[:, P:2 * P]).then_inc(rec_done, 1)

            def divide(t):
                dve.wait_ge(rec_done, t + 1)
                if t >= 2:
                    dve.wait_ge(projected, t - 1)
                nc.vector.tensor_tensor(attnT[:, t % 2, :], out_bank[:, 0:P], rec[:, t % 2, :], ALU.mult)\
                    .then_inc(attn_done, 1)

            def residual(t):
                dve.wait_ge(projected, t + 1)
                if t % HT == 0:
                    dve.wait_ge(bo_added, t // HT + 1)
                nc.vector.tensor_tensor(X1[:, t, :], projection, Xb[:, t, :], ALU.add)\
                    .then_inc(x1_done, 1)

            def stats_of(t):
                dve.wait_ge(x1_done, t + 1)
                nc.vector.bn_stats(stats2[:, t % 2, :], X1[:, t, :]).then_inc(stats2_done, 1)

            def moments_of(t):
                dve.wait_ge(stats2_done, t + 1)
                if t >= 2:
                    dve.wait_ge(xn2_done, t - 1)
                nc.vector.bn_aggr(mv2[:, t % 2, :], stats2[:, t % 2, :]).then_inc(moments2_done, 1)

            def low_x2(t):
                dve.wait_ge(x2_hi_done, t + 1)
                nc.vector.tensor_tensor(x2_lo[:, t * P:(t + 1) * P], turned_x2,
                                        x2_hi[:, t * P:(t + 1) * P].bitcast(f32), ALU.subtract)\
                    .then_inc(x2_done, 1)

            def low(r, high_done, count):
                dve.wait_ge(high_done, count)
                nc.vector.tensor_tensor(h_lo[:, r, :], score[:, r, :], h_hi[:, r, :].bitcast(f32),
                                        ALU.subtract).then_inc(h_done, 1)

            for k in range(TILES + 4):
                for j in DRAIN_LOW.get((k, FIRST), []):
                    low(j % RING, h_hi_done, j + 1)
                if 0 <= k - 3 < TILES:
                    reciprocal(k - 3)
                    divide(k - 3)
                for j in DRAIN_LOW.get((k, MIDDLE), []):
                    low(j % RING, h_hi_done, j + 1)
                if k < TILES:
                    maximum(k, 0)
                    shift(k, 0)
                if 0 <= k - 3 < TILES:
                    residual(k - 3)
                if k < TILES:
                    maximum(k, 1)
                    if k == 0:
                        low_q(1)
                    shift(k, 1)
                if 0 <= k - 3 < TILES:
                    stats_of(k - 3)
                if 0 <= k - 4 < TILES:
                    low_x2(k - 4)
                if 0 <= k - 3 < TILES:
                    moments_of(k - 3)
                if k == 0:
                    values(0)
                    dve.wait_ge(ld_bo, 16)
                    dve.wait_ge(bias_projected, 1)
                    nc.vector.tensor_tensor(bias_all[:], bias_bank, bo_all[:], ALU.add).then_inc(bias_summed, 1)
                if k == 1:
                    values(1)
                if k == 2:
                    low_q(2)
                for j in DRAIN_LOW.get((k, LAST), []):
                    low(j % RING, h_hi_done, j + 1)

            def te(ap):
                return ap.rearrange("p (t e) -> p t e", e=EXPERTS)

            def cte(ap):
                return ap.rearrange("p c (t e) -> p c t e", e=EXPERTS)

            def per_tile(ap):
                return bc(ap.unsqueeze(2), [P, TILES, EXPERTS])

            rank = bc(C("rank").unsqueeze(1), [P, TILES, EXPERTS])
            top, best, top2, best2, total, den = (r_top[:, j, :] for j in range(6))
            flat = "p c n -> p (c n)"

            def shift_logits():
                dve.wait_ge(logits_done, TILES)
                link(nc.vector.tensor_reduce(top, te(logits), AX.X, ALU.max))
                nc.vector.tensor_tensor(te(r_l[:]), te(logits), per_tile(top), ALU.subtract)\
                    .then_inc(logits_shifted, 1)

            def first_choice():
                dve.wait_ge(logits_shifted, 1)
                link(nc.vector.scalar_tensor_tensor(out=te(r_a[:]), in0=te(r_l[:]), scalar=0.0, in1=rank,
                                                    op0=ALU.is_equal, op1=ALU.mult))
                link(nc.vector.tensor_reduce(best, te(r_a[:]), AX.X, ALU.max))
                link(nc.vector.tensor_tensor(te(r_m[:, 0, :]), te(r_a[:]), per_tile(best), ALU.is_equal))

            def second_choice_a():
                link(nc.vector.scalar_tensor_tensor(out=r_b[:], in0=r_m[:, 0, :], scalar=-BIG,
                                                    in1=logits, op0=ALU.mult, op1=ALU.add))
                link(nc.vector.tensor_reduce(top2, te(r_b[:]), AX.X, ALU.max))
                link(nc.vector.tensor_tensor(te(r_a[:]), te(r_b[:]), per_tile(top2), ALU.is_equal))

            def second_choice_b():
                link(nc.vector.tensor_tensor(te(r_a[:]), te(r_a[:]), rank, ALU.mult))
                link(nc.vector.tensor_reduce(best2, te(r_a[:]), AX.X, ALU.max))
                nc.vector.tensor_tensor(te(r_m[:, 1, :]), te(r_a[:]), per_tile(best2), ALU.is_equal)\
                    .then_inc(masks_done, 1)

            def root_of_exp():
                dve.wait_ge(tanh_done, 1)
                link(nc.vector.tensor_scalar(r_c[:], r_e[:], -1.0, 1.0, ALU.mult, ALU.add))
                link(nc.vector.reciprocal(r_c[:], r_c[:]))
                nc.vector.scalar_tensor_tensor(out=r_c[:], in0=r_e[:], scalar=1.0, in1=r_c[:],
                                               op0=ALU.add, op1=ALU.mult).then_inc(root_done, 1)

            def gates_of_choices():
                dve.wait_ge(squared, 2)
                dve.wait_ge(masks_done, 1)
                link(nc.vector.tensor_reduce(total, te(r_c[:]), AX.X, ALU.add))
                link(nc.vector.tensor_tensor(cte(r_pm[:]), cte(r_m[:]),
                                             bc(te(r_c[:]).unsqueeze(1), [P, 2, TILES, EXPERTS]), ALU.mult))
                link(nc.vector.tensor_reduce(r_g[:], cte(r_pm[:]), AX.X, ALU.add))

            def weights_of_choices():
                link(nc.vector.scalar_tensor_tensor(out=den, in0=total, scalar=GATE_EPS, in1=r_g[:, 0, :],
                                                    op0=ALU.mult, op1=ALU.add))
                link(nc.vector.tensor_tensor(den, den, r_g[:, 1, :], ALU.add))
                link(nc.vector.reciprocal(den, den))
                link(nc.vector.tensor_tensor(r_g[:], r_g[:], bc(den.unsqueeze(1), [P, 2, TILES]), ALU.mult))

            def places_of_choices():
                dve.wait_ge(placed, 1)
                link(nc.vector.tensor_tensor(r_pm[:].rearrange(flat), place, r_m[:].rearrange(flat), ALU.mult))
                link(nc.vector.tensor_reduce(r_pos[:], cte(r_pm[:]), AX.X, ALU.add))
                nc.vector.scalar_tensor_tensor(out=r_g[:], in0=r_pos[:], scalar=float(CAPACITY), in1=r_g[:],
                                               op0=ALU.is_lt, op1=ALU.mult).then_inc(weights_done, 1)

            def stash(m):
                dve.wait_ge(down_done, HCH * (m + 1))
                nc.vector.tensor_scalar(y_stash[:, m, :], y_bank[m % 2][:],
                                        B("b2")[:, m % 2:m % 2 + 1], None, ALU.add).then_inc(y_stashed, 1)

            def gated(m, e, s, first):
                dve.wait_ge(down_done, m * HCH + HCH)
                if not first:
                    dve.wait_ge(y_added, m - (2 * HALVES + 1))
                nc.vector.scalar_tensor_tensor(
                    out=y_gated[:, s, :], in0=y_bank[s][:], scalar=pb[:, bass.ds(e + col_b["b2"][0], 1)],
                    in1=gate_all[:].rearrange("p e t -> p (e t)")[:, bass.ds(e * TOKENS + s * HALF, HALF)],
                    op0=ALU.add, op1=ALU.mult).then_inc(y_gated_done, 1)

            routing = {SHIFT_AT: shift_logits, FIRST_AT: first_choice, SECOND_AT: second_choice_a,
                       SECOND_AT + 2: second_choice_b, ROOT_AT: root_of_exp, GATES_AT: gates_of_choices,
                       WEIGHTS_AT: weights_of_choices, PLACES_AT: places_of_choices}
            for j in range(PAIR):
                if j >= drained(DRAIN_LOW):
                    low(j % RING, h_hi_done, j + 1)
                if j in routing:
                    routing[j]()
                if j % HCH == 1 and j > HCH:
                    stash(j // HCH - 1)

            def pair(i, first):
                for j in range(PAIR):
                    n = i * PAIR + j
                    if j % HCH == DVE_HIGH:
                        dve.wait_ge(gelu_done, n + 1)
                        dve.wait_ge(down_done, n - (RING - 1))
                        nc.vector.tensor_copy(h_hi[:, j % RING, :], score[:, j % RING, :])\
                            .then_inc(h_hi_dve_done, 1)
                        low(j % RING, h_hi_dve_done, i * DVE_HIGHS + (j // HCH + 1 - DVE_HIGHS))
                    else:
                        low(j % RING, h_hi_done, i * (PAIR - DVE_HIGHS) + (j + 1 + DVE_HIGHS - j // HCH))
                    if j == 0 and first:
                        dve.wait_ge(gate_turned, 1)
                        nc.vector.tensor_copy(gateT[:], gate_turn).then_inc(gateT_done, 1)
                    m = j // HCH - 1
                    if first and j in (HCH + 1, STEPS + HCH + 1):
                        dve.wait_ge(gate_spread[2 + j // STEPS], 16)
                    if j == 1 and first:
                        stash(2 * HALVES - 1)
                    elif j % HCH == 1:
                        gated(i * 4 + m, i * 2 + (m // HALVES), m % HALVES, first and m < HALVES)

            pair(1, True)
            for e in range(4, EXPERTS):
                dve.wait_ge(gate_spread[e], 16)
            with dve.Fori(2, EXPERTS // 2) as i:
                pair(i, False)

            def add_to_result(s, bank_, other, signal):
                nc.vector.tensor_tensor(result[:, s * HT:(s + 1) * HT, :].rearrange("p t e -> p (t e)"), bank_[:],
                                        other[:, s * HT:(s + 1) * HT, :].rearrange("p t e -> p (t e)"), ALU.add)\
                    .then_inc(signal, 1)

            for s in range(HALVES):
                dve.wait_ge(final_done, s + 1)
                add_to_result(s, final_bank[s], X1, result_done if s == 0 else result_begun)
            dve.wait_ge(down_done, EXPERTS * STEPS)
            dve.wait_ge(y_added, 2 * EXPERTS - 2 * HALVES - 2)
            for w in range(2):
                piece = slice(w * PIECE, (w + 1) * PIECE)
                nc.vector.scalar_tensor_tensor(
                    out=y_gated[:, 1, piece], in0=y_bank[1][:, piece], scalar=B("b2")[:, EXPERTS - 1:EXPERTS],
                    in1=gate_all[:, EXPERTS - 1, HALF + w * PIECE:HALF + (w + 1) * PIECE],
                    op0=ALU.add, op1=ALU.mult).then_inc(piece_gated, 1)
            dve.wait_ge(result_begun, 1)
            for w in range(2):
                dve.wait_ge(final_done, HALVES + w + 1)
                piece = result[:, HT + w * HT // 2:HT + (w + 1) * HT // 2, :].rearrange("p t e -> p (t e)")
                nc.vector.tensor_tensor(piece, last_bank[w][:, 0:PIECE], piece, ALU.add).then_inc(result_done, 1)

        @block.tensor
        def _(pe):
            mm, turn = nc.tensor.matmul, nc.tensor.transpose
            ident = C("ident")

            def three(o, w_hi, w_lo, m_hi, m_lo, start, stop):
                mm(o, w_lo, m_hi, start=start, stop=False)
                mm(o, w_hi, m_lo, start=False, stop=False)
                return mm(o, w_hi, m_hi, start=False, stop=stop)

            def turn_norm(n):
                a, b = Q_PIECES[n]
                for t in range(a // P, b // P):
                    if t < HT:
                        pe.wait_ge(normed, t + 1)
                    else:
                        pe.wait_ge(normed_late, t - HT + 1)
                    last = turn(norm_piece(n)[:, t * P - a:(t + 1) * P - a], xn[:, t, :], ident)
                last.then_inc(norm_turned, 1)

            def project_q(n):
                a, b = Q_PIECES[n]
                pe.wait_ge(norm_copied, n + 1)
                mm(q_piece(n), B("wq"), xnT[:, a:b], start=True, stop=True).then_inc(q_projected, 1)

            def project_v(b):
                pe.wait_ge(ctx_copied, b + 1)
                if b == 0:
                    pe.wait_ge(zeros_set, 1)
                    pe.wait_ge(kt_done, 1)
                else:
                    pe.wait_ge(q_done, 1)
                for r in range(GCHUNKS):
                    last = mm(values_bank[b][:, r * EMB:(r + 1) * EMB], ctx_rep[:, b, r * P:(r + 1) * P],
                              A("wv"), start=True, stop=True)
                last.then_inc(values_projected, 1)

            def keep_warm(n):
                for _ in range(n):
                    mm(score[:, 0, :], warm[:, 0:P], warm[:], start=True, stop=True)

            pe.wait_ge(warm_set, 1)
            keep_warm(WARM_UP)
            pe.wait_ge(ld_pa, 16)
            mm(mixed_bank[:, 0:BATCH * KEYS], A("wk"), A("ctx"), start=True, stop=True)\
                .then_inc(keys_projected, 1)
            keep_warm(4)
            pe.wait_ge(ld_cst, 16)
            turn_norm(0)
            keep_warm(2)
            pe.wait_ge(ld_pb, 16)
            project_q(0)
            turn_norm(1)
            keep_warm(2)

            def scores(t):
                b, tt = t // BATCH_TILES, slice(t * P, (t + 1) * P)
                for a in range(2):
                    if t >= 1:
                        pe.wait_ge(shift_done, 2 * (t - 1) + a + 1)
                    for n, (w, m) in enumerate(((q_lo, kb_hi), (q_hi, kb_lo), (q_hi, kb_hi))):
                        for g in (2 * a, 2 * a + 1):
                            rows = slice(32 * g, 32 * (g + 1))
                            last = mm(score[:, g, 0:GCOLS], w[rows, tt], m[rows, b, :],
                                      start=(n == 0), stop=(n == 2))
                    last.then_inc(scored, 1)

            def turns(t, quads):
                for j in quads:
                    c0, c1 = j * QUAD, (j + 1) * QUAD
                    u = QUADS * t + j
                    pe.wait_ge(shift_done, 2 * t + (1 if c1 * P <= 2 * GWIDTH else 2))
                    if u >= 2:
                        pe.wait_ge(exp_done, u - 1)
                    for c in range(c0, c1):
                        last = turn(turned_bank[u % 2][:, (c - c0) * P:(c - c0 + 1) * P],
                                    shifted[:, t % 2, c * P:(c + 1) * P], ident)
                    last.then_inc(turned, 1)

            def weigh(t):
                b = t // BATCH_TILES
                if t >= 1:
                    pe.wait_ge(x1_done, t)
                pe.wait_ge(exp_done, QUADS * (t + 1))
                for what, col in ((v_ones, P), (v_blk, 0)):
                    for r in range(GCHUNKS):
                        for g in range(GROUPS):
                            c = g * GCHUNKS + r
                            w = v_ones[:, r, :] if what is v_ones else v_blk[:, b, r, 32 * g:32 * (g + 1)]
                            last = mm(out_bank[32 * g:32 * (g + 1), col:col + P], w,
                                      probs[:, t % 2, c * P:(c + 1) * P],
                                      start=(r == 0), stop=(r == GCHUNKS - 1))
                last.then_inc(weighted, 1)

            def project(t):
                pe.wait_ge(attn_done, t + 1)
                mm(projection, attnT[:, t % 2, :], B("wo"), start=True, stop=True).then_inc(projected, 1)

            def turn_x2(t):
                pe.wait_ge(xn2_done, t + 1)
                if t >= 1:
                    pe.wait_ge(x2_done, t)
                turn(turned_x2, xn2[:, t % 2, :], ident).then_inc(xn2_turned, 1)

            def project_logits(t):
                pe.wait_ge(x2_done, t + 1)
                tt = slice(t * P, (t + 1) * P)
                three(logits[:, t * EXPERTS:(t + 1) * EXPERTS], x2_hi[:, tt], x2_lo[:, tt],
                      wg_hi[:], wg_lo[:], True, True).then_inc(logits_done, 1)

            def up(n, u, s, c, r, first):
                if not first:
                    pe.wait_ge(h_done, n - (RING - 1))
                cc, ss = slice(c * P, (c + 1) * P), slice(s * HALF, (s + 1) * HALF)
                three(score[:, r, :], w1_hi[:, u, cc], w1_lo[:, u, cc], x2_hi[:, ss], x2_lo[:, ss],
                      True, True).then_inc(up_done, 1)

            def down(n, u, s, c, r, first):
                pe.wait_ge(h_done, n + 1)
                cc = slice(c * P, (c + 1) * P)
                three(y_bank[s][:], w2_hi[:, u, cc], w2_lo[:, u, cc], h_hi[:, r, :], h_lo[:, r, :],
                      c == 0, c == HCH - 1).then_inc(down_done, 1)

            def step_up(i, j, first):
                if j % STEPS == 0:
                    pe.wait_ge(w1_split, i * 2 + (j // STEPS + 1))
                up(i * PAIR + j, j // STEPS % 2, j // HCH % HALVES, j % HCH, j % RING, first)

            def step_up_0(j):
                if j >= PAIR:
                    step_up(0, j, False)
                    return
                if j in (0, HCH):
                    pe.wait_ge(w1_split, expert_0(j) + 1)
                up(j, expert_0(j), half_0(j), j % HCH, j % RING, j < RING)

            def step_down_0(j):
                m = j // HCH
                if j in (0, HCH):
                    pe.wait_ge(w2_split, expert_0(j) + 1)
                if j == 0:
                    pe.wait_ge(exp_done, QUADS * TILES)
                if j % HCH == 0 and m >= 2:
                    pe.wait_ge(y_stashed, m - 1)
                down(j, expert_0(j), m % 2, j % HCH, j % RING, j < RING)

            def step_down(i, j, stashed, first):
                m = j // HCH
                if j % STEPS == 0:
                    pe.wait_ge(w2_split, i * 2 + (j // STEPS + 1))
                if j % HCH == 0:
                    if stashed > 0:
                        pe.wait_ge(y_stashed, stashed)
                    elif not first:
                        pe.wait_ge(y_gated_done, i * 4 + (m - 1 - 2 * HALVES))
                down(i * PAIR + j, j // STEPS, m % HALVES, j % HCH, j % RING, first)

            def steps_of_experts(at):
                if at == (TILES, FIRST):
                    pe.wait_ge(shift_done, 2 * TILES)
                for j in DRAIN_UP.get(at, []):
                    step_up_0(j)
                for j in DRAIN_DOWN.get(at, []):
                    step_down_0(j)

            for k in range(TILES + 4):
                if k < TILES:
                    b = k // BATCH_TILES
                    if k % BATCH_TILES == 0:
                        pe.wait_ge(kb_hi_done, GH * (b + 1))
                        pe.wait_ge(kb_lo_done, GH * (b + 1))
                    pe.wait_ge(q_done, 1 if k == 0 else 2 + b)
                    scores(k)
                if k == 2:
                    project_q(2)
                if k == 0:
                    project_q(1)
                    project_v(0)
                    project_v(1)
                    pe.wait_ge(bv_spread, 1)
                    mm(bias_bank, bv_rep[:], B("wo"), start=True, stop=True).then_inc(bias_projected, 1)
                if 0 <= k - 1 < TILES:
                    if k == 1:
                        pe.wait_ge(norm_copied, 2)
                        pe.wait_ge(q_done, 2)
                    turns(k - 1, (0, 1))
                if k == LOGITS_LAG:
                    pe.wait_ge(wg_done, 1)
                if LOGITS_LAG <= k <= TILES:
                    project_logits(k - LOGITS_LAG)
                steps_of_experts((k, FIRST))
                if 0 <= k - 4 < TILES:
                    if k == 4:
                        pe.wait_ge(q_done, 3)
                    turn_x2(k - 4)
                if 0 <= k - 3 < TILES:
                    project(k - 3)
                steps_of_experts((k, MIDDLE))
                if 0 <= k - 1 < TILES:
                    turns(k - 1, (2,))
                if 0 <= k - 2 < TILES:
                    if k == 2:
                        pe.wait_ge(values_set, BATCH)
                        pe.wait_ge(v_ones_set, 1)
                        pe.wait_ge(bias_summed, 1)
                    weigh(k - 2)
                if k >= TILES:
                    project_logits(k - 4)
                if k == 1:
                    pe.wait_ge(values_set, 1)
                    turn_norm(2)
                steps_of_experts((k, LAST))

            def place_choices():
                pe.wait_ge(masks_done, 1)
                pe.wait_ge(upper_set, 1)
                pe.wait_ge(consts_set, 2)
                place4 = place.rearrange("p (c t e) -> p c t e", c=2, e=EXPERTS)
                masks = r_m[:].rearrange("p c (t e) -> p c t e", e=EXPERTS)
                mm(place, upper_bf[:], r_m[:].rearrange("p c n -> p (c n)"), start=True, stop=False)
                for d in range(1, TILES):
                    mm(place4[:, :, d:TILES, :], ones_bf[:], masks[:, :, 0:TILES - d, :],
                       start=False, stop=False)
                for t in range(TILES):
                    last = mm(place4[:, 1], ones_bf[:],
                              masks[:, 0, t:t + 1, :].broadcast_to([P, TILES, EXPERTS]),
                              start=False, stop=(t == TILES - 1))
                last.then_inc(placed, 1)

            def turn_gates():
                pe.wait_ge(gate_done, 1)
                turn(gate_turn, gate[:], ident).then_inc(gate_turned, 1)

            ups = drained(DRAIN_UP)
            for j in range(drained(DRAIN_DOWN), PAIR):
                for n in range(ups, j + AHEAD + 1):
                    step_up_0(n)
                ups = max(ups, j + AHEAD + 1)
                step_down_0(j)
                if j == PLACE_AT:
                    place_choices()
                if j == TURN_AT:
                    turn_gates()
            for j in range(PAIR):
                step_up(1, j + AHEAD, False)
                m = j // HCH
                step_down(1, j, 2 * HALVES - 1 + m if m < HALVES else 0, m < HALVES)
            with pe.Fori(2, EXPERTS // 2 - 1) as i:
                for j in range(PAIR):
                    step_up(i, j + AHEAD, False)
                    step_down(i, j, 0, False)

            def turn_sum(s):
                for t in range(HT):
                    last = turn(final_bank[s][:, t * P:(t + 1) * P],
                                y_sum[:, s * HALF + t * P:s * HALF + (t + 1) * P], ident)
                last.then_inc(final_done, 1)

            for j in range(PAIR):
                if j + AHEAD < PAIR:
                    step_up(EXPERTS // 2 - 1, j + AHEAD, False)
                step_down(EXPERTS // 2 - 1, j, 0, False)
                if j == PAIR - 2:
                    pe.wait_ge(stash_added, 2 * HALVES)
                    pe.wait_ge(gate_turned, 1)
                    pe.wait_ge(y_added, 2 * EXPERTS - 2 * HALVES - 1)
                    for s in range(HALVES):
                        turn_sum(s)
            pe.wait_ge(h_done, EXPERTS * STEPS)
            for w in range(2):
                pe.wait_ge(piece_gated, w + 1)
                for t in range(HT // 2):
                    last = turn(last_bank[w][:, t * P:(t + 1) * P],
                                y_gated[:, 1, w * PIECE + t * P:w * PIECE + (t + 1) * P], ident)
                last.then_inc(final_done, 1)


def constants():
    import numpy as np
    ident = np.eye(P)
    head = np.arange(P)[:, None] // HEAD_DIM % GH == np.arange(GH)[None, :]
    row = np.arange(GCHUNKS)[None, :] * P + np.arange(P)[:, None]
    vmask = (row[:, :, None] // KEYS == np.arange(GH)).reshape(P, GCHUNKS * GH)
    upper = np.arange(P)[:, None] < np.arange(P)[None, :]
    rank = np.broadcast_to(EXPERTS - np.arange(EXPERTS), (P, EXPERTS))
    return np.concatenate([ident, head, vmask, upper, rank], axis=1).astype(np.float32)


def kernel(x, ctx_1024, mask_BxSxS2_if1, L0_xattn_Wq, L0_xattn_bq, L0_xattn_Wk, L0_xattn_bk,
           L0_xattn_Wv, L0_xattn_bv, L0_xattn_Wo, L0_xattn_bo, L0_ffn_Wg, L0_ffn_W1, L0_ffn_b1,
           L0_ffn_W2, L0_ffn_b2):
    import numpy as np
    import concourse.bacc as bacc
    from concourse.bass_utils import run_bass_kernel_spmd

    a = np.asarray
    ctx_t = a(ctx_1024).reshape(BATCH * KEYS, EMB).T
    par_a = np.concatenate([a(L0_xattn_Wk).T, ctx_t, a(L0_xattn_Wv).T, a(L0_xattn_bk)[:, None],
                            a(L0_xattn_bq)[:, None], a(L0_xattn_bv)[:, None]], axis=1)
    par_b = np.concatenate([a(L0_xattn_Wq).T, a(L0_xattn_Wo).T, a(L0_ffn_Wg),
                            a(L0_ffn_b1).reshape(EXPERTS * HCH, P).T, a(L0_ffn_b2).T], axis=1)
    arrays = {
        "x": a(x).reshape(TOKENS, EMB), "par_a": par_a, "par_b": par_b,
        "bias_o": a(L0_xattn_bo), "w1": a(L0_ffn_W1), "w2": a(L0_ffn_W2),
        "const": constants(),
    }
    arrays = {f"in_{k}": np.ascontiguousarray(v) for k, v in arrays.items()}
    nc = bacc.Bacc("TRN2", target_bir_lowering=False, num_devices=1)
    args = [nc.dram_tensor(k, v.shape, mybir.dt.from_np(v.dtype), kind="ExternalInput").ap()
            for k, v in arrays.items()]
    args.append(nc.dram_tensor("out_0", (TOKENS, EMB), mybir.dt.float32, kind="ExternalOutput").ap())
    xattn_moe(nc, *args)
    r = run_bass_kernel_spmd(nc, [arrays], core_ids=[0])
    return r.results[0]["out_0"].reshape(BATCH, SEQ, EMB)
```
